# Optimizing a Trainium2 kernel written in Bass

```python
import numpy as np
import jax
import jax.numpy as jnp

def _softmax(x, axis=-1):
    return jax.nn.softmax(x, axis=axis)

def _gelu(x):
    return jax.nn.gelu(x, approximate=True)

def _silu(x):
    return jax.nn.silu(x)

def _sigmoid(x):
    return jax.nn.sigmoid(x)

def _layernorm(x, axis=-1, eps=1e-05):
    m = jnp.mean(x, axis=axis, keepdims=True)
    v = jnp.var(x, axis=axis, keepdims=True)
    return (x - m) / jnp.sqrt(v + eps)

def _scatter_add(tgt, idx, src, axis=0):
    return tgt.at[idx].add(src)

def _segment_sum(src, seg, n):
    return jax.ops.segment_sum(src, seg, n)
kernel_name = 'mk_adj_preln_d2_adj_r2_7979e3'

def setup_inputs(seed: int=0):
    np.random.seed(seed)
    _w = jnp.asarray

    def _rec_inputs():
        import jax
        import jax.numpy as jnp
        _gk = jax.random.key(seed)
        x = -0.0004039 + 1 * jax.random.normal(jax.random.fold_in(_gk, 1), (16, 512, 384), jnp.float32)
        _w = (1.0 + jnp.arange(512, dtype=jnp.float32)) ** (-0.5)
        _w = _w / _w.mean()
        _pij = jnp.clip(0.03125 * _w[:, None] * _w[None, :], 0.0, 1.0)
        _a = jax.random.uniform(jax.random.fold_in(_gk, 2), (16, 512, 512)) < _pij
        _af = _a.astype(jnp.float32)
        adj = _af
        return (x, adj)
    x, adj = _rec_inputs()

    def _L0_gnn_setup():
        import jax, jax.numpy as jnp
        import numpy as np
        B, S, H, L = (32, 256, 384, 2)

        def _layer_norm(z, a, b, eps=0.001):
            mu = jnp.mean(z, axis=-1, keepdims=True)
            sigma = jnp.std(z, axis=-1, keepdims=True, ddof=1)
            return (z - mu) / (sigma + eps) * a + b
        key = jax.random.key(seed)
        ks = jax.random.split(key, 6)
        hidden_state = jax.random.normal(ks[0], (B, S, H), dtype=jnp.float32)
        adjacency_matrix = (jax.random.uniform(ks[1], (B, S, S)) < 0.2).astype(jnp.float32)
        W_left = 0.05 * jax.random.normal(ks[2], (L, H, H), dtype=jnp.float32)
        W_right = 0.05 * jax.random.normal(ks[3], (L, H, H), dtype=jnp.float32)
        W_lin = 0.05 * jax.random.normal(ks[4], (L, H, H), dtype=jnp.float32)
        b_lin = jnp.zeros((L, H), dtype=jnp.float32)
        ln_a = jnp.ones((L, H), dtype=jnp.float32)
        ln_b = jnp.zeros((L, H), dtype=jnp.float32)
        return {'hidden_state': hidden_state, 'adjacency_matrix': adjacency_matrix, 'W_left': W_left, 'W_right': W_right, 'W_lin': W_lin, 'b_lin': b_lin, 'ln_a': ln_a, 'ln_b': ln_b}
    _L0_gnn_all = _L0_gnn_setup()
    _L0_gnn_in = {k: v for k, v in _L0_gnn_all.items() if k in ('W_left', 'W_right', 'W_lin', 'b_lin', 'ln_a', 'ln_b')}
    del _L0_gnn_all

    def _L1_gnn_setup():
        import jax, jax.numpy as jnp
        import numpy as np
        B, L, H = (8, 1024, 384)
        LN_EPS = 1e-12
        key = jax.random.key(seed)
        ks = jax.random.split(key, 10)
        hidden_state = jax.random.normal(ks[0], (B, L, H), dtype=jnp.float32)
        adjacency = jax.random.randint(ks[1], (B, L, L), 0, 2).astype(jnp.float32)
        bound = 1.0 / np.sqrt(H)
        W_left = jax.random.normal(ks[2], (H, H), dtype=jnp.float32) * np.sqrt(2.0 / (H + H))
        b_left = jax.random.uniform(ks[3], (H,), minval=-bound, maxval=bound, dtype=jnp.float32)
        W_self = jax.random.normal(ks[4], (H, H), dtype=jnp.float32) * np.sqrt(2.0 / (H + H))
        b_self = jax.random.uniform(ks[5], (H,), minval=-bound, maxval=bound, dtype=jnp.float32)
        W_right = jax.random.normal(ks[6], (H, H), dtype=jnp.float32) * np.sqrt(2.0 / (H + H))
        b_right = jax.random.uniform(ks[7], (H,), minval=-bound, maxval=bound, dtype=jnp.float32)
        gamma = jnp.ones((H,), dtype=jnp.float32)
        beta = jnp.zeros((H,), dtype=jnp.float32)
        return {'hidden_state': hidden_state, 'adjacency': adjacency, 'W_left': W_left, 'b_left': b_left, 'W_self': W_self, 'b_self': b_self, 'W_right': W_right, 'b_right': b_right, 'gamma': gamma, 'beta': beta}
    _L1_gnn_all = _L1_gnn_setup()
    _L1_gnn_in = {k: v for k, v in _L1_gnn_all.items() if k in ('W_left', 'b_left', 'W_self', 'b_self', 'W_right', 'b_right', 'gamma', 'beta')}
    del _L1_gnn_all
    return {'x': x, 'adj': adj, 'L0_gnn_W_left': _L0_gnn_in['W_left'], 'L0_gnn_W_right': _L0_gnn_in['W_right'], 'L0_gnn_W_lin': _L0_gnn_in['W_lin'], 'L0_gnn_b_lin': _L0_gnn_in['b_lin'], 'L0_gnn_ln_a': _L0_gnn_in['ln_a'], 'L0_gnn_ln_b': _L0_gnn_in['ln_b'], 'L1_gnn_W_left': _L1_gnn_in['W_left'], 'L1_gnn_b_left': _L1_gnn_in['b_left'], 'L1_gnn_W_self': _L1_gnn_in['W_self'], 'L1_gnn_b_self': _L1_gnn_in['b_self'], 'L1_gnn_W_right': _L1_gnn_in['W_right'], 'L1_gnn_b_right': _L1_gnn_in['b_right'], 'L1_gnn_gamma': _L1_gnn_in['gamma'], 'L1_gnn_beta': _L1_gnn_in['beta']}

def reference(x, adj, L0_gnn_W_left, L0_gnn_W_right, L0_gnn_W_lin, L0_gnn_b_lin, L0_gnn_ln_a, L0_gnn_ln_b, L1_gnn_W_left, L1_gnn_b_left, L1_gnn_W_self, L1_gnn_b_self, L1_gnn_W_right, L1_gnn_b_right, L1_gnn_gamma, L1_gnn_beta):
    import jax
    import jax.numpy as jnp

    def _L0_gnn_ref(hidden_state, adjacency_matrix, W_left, W_right, W_lin, b_lin, ln_a, ln_b):
        import jax, jax.numpy as jnp
        import numpy as np
        B, S, H, L = (32, 256, 384, 2)

        def _layer_norm(z, a, b, eps=0.001):
            mu = jnp.mean(z, axis=-1, keepdims=True)
            sigma = jnp.std(z, axis=-1, keepdims=True, ddof=1)
            return (z - mu) / (sigma + eps) * a + b
        temper = float(np.sqrt(H))
        adj = adjacency_matrix
        adj_tri = jnp.triu(adj, k=1)
        diag_mask = jnp.triu(adj, k=0) - adj_tri
        h = hidden_state
        for l in range(L):
            m_left = jnp.einsum('bsh,oh->bso', h, W_left[l])
            m_right = jnp.einsum('bsh,oh->bso', h, W_right[l])
            u_left = jnp.einsum('bih,bjh->bij', h, m_left) / temper
            u_right = jnp.einsum('bih,bjh->bij', h, m_right) / temper
            u = u_left * adj_tri + u_left * diag_mask + u_right * jnp.swapaxes(adj_tri, 1, 2)
            delta_exp_u = jnp.exp(u) * adj
            attention = delta_exp_u / (jnp.sum(delta_exp_u, axis=2, keepdims=True) + 1e-10)
            h_lin = jnp.einsum('bsh,oh->bso', h, W_lin[l]) + b_lin[l]
            ctx = jnp.matmul(attention, h_lin)
            h = jax.nn.relu(_layer_norm(ctx, ln_a[l], ln_b[l]))
        return h

    def _L1_gnn_ref(hidden_state, adjacency, W_left, b_left, W_self, b_self, W_right, b_right, gamma, beta):
        import jax, jax.numpy as jnp
        import numpy as np
        B, L, H = (8, 1024, 384)
        LN_EPS = 1e-12
        h = hidden_state
        d = h.shape[-1]
        n = h.shape[1]
        u = jnp.einsum('bld,bmd->blm', h, h) / jnp.sqrt(jnp.asarray(d, h.dtype))
        p = jax.nn.softmax(u, axis=-1)
        delta = p * adjacency
        attn = delta / (jnp.sum(delta, axis=2, keepdims=True) + 1e-10)
        h_left = jnp.einsum('bld,ed->ble', h, W_left) + b_left
        h_self = jnp.einsum('bld,ed->ble', h, W_self) + b_self
        h_right = jnp.einsum('bld,ed->ble', h, W_right) + b_right
        i = jnp.arange(n)[:, None]
        j = jnp.arange(n)[None, :]
        attn_left = jnp.where(j > i, attn, 0.0)
        attn_right = jnp.where(j < i, attn, 0.0)
        diag_a = jnp.diagonal(attn, axis1=1, axis2=2)
        ctx = jnp.einsum('blm,bmd->bld', attn_left, h_left) + diag_a[..., None] * h_self + jnp.einsum('blm,bmd->bld', attn_right, h_right)
        mu = jnp.mean(ctx, axis=-1, keepdims=True)
        var = jnp.mean(jnp.square(ctx - mu), axis=-1, keepdims=True)
        o = (ctx - mu) / jnp.sqrt(var + LN_EPS) * gamma + beta
        return jax.nn.relu(o)
    h = jnp.maximum(_layernorm(x, axis=-1), 0.0)
    x = x + _L0_gnn_ref(h, adj, L0_gnn_W_left, L0_gnn_W_right, L0_gnn_W_lin, L0_gnn_b_lin, L0_gnn_ln_a, L0_gnn_ln_b)
    h = jnp.maximum(_layernorm(x, axis=-1), 0.0)
    x = x + _L1_gnn_ref(h, adj, L1_gnn_W_left, L1_gnn_b_left, L1_gnn_W_self, L1_gnn_b_self, L1_gnn_W_right, L1_gnn_b_right, L1_gnn_gamma, L1_gnn_beta)
    return x

_drawn_inputs = setup_inputs


def setup_inputs(seed=0):
    import zlib

    import numpy as np

    out = dict(_drawn_inputs(seed))
    spreads = {'L0_gnn_b_lin': (0.0, 0.1),
     'L0_gnn_ln_a': (1.0, 0.2),
     'L0_gnn_ln_b': (0.0, 0.1),
     'L1_gnn_gamma': (1.0, 0.2),
     'L1_gnn_beta': (0.0, 0.1)}
    factors = {'L0_gnn_W_left': 3.711,
     'L0_gnn_W_right': 8.0,
     'L1_gnn_b_left': 4.66,
     'L1_gnn_b_self': 8.0,
     'L1_gnn_b_right': 2.847}
    for name, (base, spread) in spreads.items():
        noise = np.random.default_rng([zlib.crc32(name.encode()), seed]).standard_normal(out[name].shape)
        drawn = base * np.exp(spread * noise) if base else spread * noise
        out[name] = jnp.asarray(drawn.astype(out[name].dtype))
    for name, factor in factors.items():
        out[name] = (out[name] * factor).astype(out[name].dtype)
    return out
```

```python
from contextlib import ExitStack

import concourse.bass as bass
from concourse import mybir

F32 = mybir.dt.float32
F32R = mybir.dt.float32r
I32 = mybir.dt.int32
ALU = mybir.AluOpType
ACT = mybir.ActivationFunctionType
AX_X = mybir.AxisListType.X

P = 128
B, S, H = 16, 512, 384
NB = S // P
NC = H // P
VW = H + 2
DW = S + P
STEPS = 6
ROUNDS = B // 2
ROOT_H = float(H) ** -0.5
MIN_N = 256
NEG_HALF_MAGIC = float(0x5F3759DF)


def job_table():
    table, frees, n = {}, {}, 0
    for s in range(STEPS):
        z = [("z", 1)] if s in (0, 5) else []
        if s < 4:
            order = [("ml", NC), ("mr", NC)] + z + [("c", NB), ("hl", NB), ("t", NC)]
        else:
            order = [("hl", NB)] + z + [("c", NB), ("hr", NB), ("hs", NB)]
        for name, count in order:
            for k in range(count):
                table[s, name, k] = n
                n += 1
                if name != "t":
                    frees[s, name, k] = len(frees)
    return table, n, frees


JOBS, JOBS_PER_ROUND, FREES = job_table()
JOB_AT = {n: key for key, n in JOBS.items()}
HL_BEFORE = [4 * s if s < 4 else 16 + 8 * (s - 4) for s in range(STEPS)]
PHI_BEFORE = [10 * s if s < 4 else 40 + 8 * (s - 4) for s in range(STEPS)]


def gnn_kernel(nc, x_in, adj_in, adjt_in, w_in, vec_in, lnab_in, out):
    with ExitStack() as ctx:
        def sb(name, shape, dt=F32):
            return ctx.enter_context(nc.sbuf_tensor(name, shape, dt))

        def sem(name):
            return ctx.enter_context(nc.semaphore(name))

        ring = [ctx.enter_context(nc.psum_tensor(f"ring{k}", [P, 512], F32)) for k in range(4)]
        score = [ctx.enter_context(nc.psum_tensor(f"score{k}", [P, 512], F32)) for k in range(4)]

        w_stage = sb("w_stage", [P, NC, H])
        w_hi = sb("w_hi", [P, 3, NC, H], F32R)
        w_lo = sb("w_lo", [P, 3, NC, H], F32R)
        vec = sb("vec", [P, 9, H])
        lnab = sb("lnab", [P, 2, NC])
        ht_hi = sb("ht_hi", [P, NC, S], F32R)
        ht_lo = sb("ht_lo", [P, NC, S], F32R)
        mix = sb("mix", [P, 4 * NC * S], F32R)
        ml_hi, ml_lo, mr_hi, mr_lo = (
            mix[:, q * NC * S:(q + 1) * NC * S].rearrange("p (c s) -> p c s", c=NC) for q in range(4))
        hl_hi = [sb(f"hl_hi{x}", [P, NB, VW], F32R) for x in range(2)]
        hl_lo = [sb(f"hl_lo{x}", [P, NB, VW], F32R) for x in range(2)]
        hrb = sb("hrb", [P, 2 * NB * VW], F32R)
        hr_hi, hr_lo = ([r[:, q * NB * VW:(q + 1) * NB * VW].rearrange("p (b v) -> p b v", b=NB)
                         for r in (mix, hrb)] for q in range(2))
        d_hi = sb("d_hi", [P, NB, DW], F32R)
        d_lo = sb("d_lo", [P, NB, DW], F32R)
        adjt = [sb(f"adjt{x}", [P, NB, S]) for x in range(2)]
        adjn = [sb(f"adjn{x}", [P, NB * H]) for x in range(2)]
        hs = [adjn[x][:, :].rearrange("p (b v) -> p b v", b=NB) for x in range(2)]
        AT = [sum(S - P * k for k in range(J)) for J in range(NB + 1)]
        xres = [sb(f"xres{x}", [P, NB, H]) for x in range(2)]
        xnext = sb("xnext", [P, NB, H])
        xhat = sb("xhat", [P, NB, H])
        td = sb("td", [P, 3, DW])
        esum = sb("esum", [P, S])
        pt = sb("pt", [P, 2, S])
        negmax = sb("negmax", [P, NB, P], F32R)
        ident = sb("ident", [P, P])
        low = sb("low", [P, P])
        below = sb("below", [P, P])
        above = sb("above", [P, P])
        ones_r = sb("ones_r", [P, P], F32R)
        ones = ones_r[:, :].bitcast(F32)
        stats = sb("stats", [P, NB, 6])
        small = sb("small", [P, 12, NB])
        den, rden, var, rs, nb, nt, mx, zc, ddr, msum = (small[:, k, :] for k in range(10))
        diag = small[:, 10:12, :]
        junk = pt

        const_done = sem("const_done")
        vec_in_sem = sem("vec_in_sem")
        w_raw = sem("w_raw")
        xnext_in = sem("xnext_in")
        xres_in = [sem(f"xres_in{x}") for x in range(2)]
        adj_in_sem = [sem(f"adj_in{x}") for x in range(2)]
        w_split_hi = sem("w_split_hi")
        w_split_lo = sem("w_split_lo")
        ring_full = sem("ring_full")
        ring_free = sem("ring_free")
        xhat_ready = sem("xhat_ready")
        ht_pre = sem("ht_pre")
        ht_hi_done = sem("ht_hi_done")
        ht_lo_done = sem("ht_lo_done")
        ht_free = sem("ht_free")
        ts_full = sem("ts_full")
        proj_hi = sem("proj_hi")
        val_lo = sem("val_lo")
        score_full = sem("score_full")
        masked = sem("masked")
        exp_done = sem("exp_done")
        esum_done = sem("esum_done")
        weight_done = sem("weight_done")
        weight_hi = sem("weight_hi")
        weight_lo = sem("weight_lo")
        max_ready = sem("max_ready")
        max_added = sem("max_added")
        adjn_ready = sem("adjn_ready")
        out_ready = [sem(f"out_ready{x}") for x in range(2)]
        out_done = [sem(f"out_done{x}") for x in range(2)]
        dve_chain = sem("dve_chain")
        pool_chain = sem("pool_chain")

        def left_out(i):
            return 2 * NC if isinstance(i, int) and i == ROUNDS else 0

        def job(i, s, name, k=0):
            return i * JOBS_PER_ROUND + (JOBS[s, name, k] + 1 - left_out(i))

        def freed(i, s, name, k=0):
            return i * len(FREES) + (FREES[s, name, k] + 1 - left_out(i))

        def bank(s, name, k=0):
            return ring[JOBS[s, name, k] % 4]

        def step_count(i, s, per, k=0):
            return i * (STEPS * per) + (s * per + k + 1)

        def late(i, s):
            return not (isinstance(i, int) and i == 0 and s == 0)

        def wait_ht_free(eng, g_i, g_s, k):
            if isinstance(g_i, int) and g_i == 0 and g_s == 0:
                return
            if k < NC - 1:
                eng.wait_ge(ht_free, g_i * (2 * STEPS) + (2 * g_s - 2 + k + 1))
            elif g_s == 0:
                eng.wait_ge(ring_full, g_i * JOBS_PER_ROUND)
            elif g_s == 5:
                eng.wait_ge(ring_full, job(g_i, 4, "hs", NB - 1))
            else:
                eng.wait_ge(score_full, step_count(g_i, g_s - 1, 4, 3))

        def w_index(i, s, slot):
            return i * 9 + (3 * (s // 2) + slot)

        def xrows(i, x):
            return x_in[bass.ds(i, 1), :, :].rearrange("a (b p) h -> p (a b) h", p=P)

        block = ctx.enter_context(nc.Block())

        @block.sync
        def _(sp):
            def load_w(i, s, slot, ahead):
                n = w_index(i, s, slot)
                if not (isinstance(n, int) and n == 0):
                    sp.wait_ge(w_split_lo, n)
                layer = (s // 2) % 3
                sp.dma_start(w_stage[:, :, :], w_in[layer, slot].rearrange("(c p) o -> p c o", p=P)).then_inc(w_raw, 16)

            def load_adj(b, x):
                sp.dma_start(adjt[x][:, :, :],
                             adjt_in[bass.ds(b, 1), :, :].rearrange("a (b p) s -> p (a b) s", p=P)).then_inc(adj_in_sem[x], 16)
                for J in range(NB):
                    sp.dma_start(adjn[x][:, AT[J]:AT[J + 1]],
                                 adj_in[bass.ds(b, 1), J * P:(J + 1) * P, J * P:S].rearrange("a p s -> (a p) s")
                                 ).then_inc(adj_in_sem[x], 16)

            def load_xnext(b):
                sp.dma_start(xnext[:, :, :], xrows(b, 0)).then_inc(xnext_in, 16)

            def load_xres(b, x):
                sp.dma_start(xres[x][:, :, :], xrows(b, x)).then_inc(xres_in[x], 16)

            def store(b, x):
                sp.dma_start(out[bass.ds(b, 1), :, :].rearrange("a (b p) h -> p (a b) h", p=P),
                             xres[x][:, :, :]).then_inc(out_done[x], 16)

            def round_of_loads(i, last):
                if late(i, 0):
                    sp.wait_ge(out_ready[1], i)
                    store(i * 2 - 1, 1)
                    sp.wait_ge(weight_done, i * 24)
                    load_adj(i * 2 + 1, 1)
                    sp.wait_ge(out_done[1], i * 16)
                    load_xres(i * 2 + 1, 1)
                load_w(i, 0, 2, 0)
                load_w(i, 2, 0, 0)
                load_w(i, 2, 1, 0)
                sp.wait_ge(ring_full, job(i, 0, "t", 2))
                load_xnext(0 if last else i * 2 + 2)
                load_w(i, 2, 2, 0)
                load_w(i, 4, 0, 0)
                load_w(i, 4, 1, 0)
                load_w(i, 4, 2, 0)
                load_w(i, 6, 0, 0)
                load_w(i, 6, 1, 0)
                sp.wait_ge(out_ready[0], i + 1)
                store(i * 2, 0)
                if not last:
                    sp.wait_ge(weight_done, i * 24 + 20)
                    load_adj(i * 2 + 2, 0)
                    sp.wait_ge(out_done[0], i * 16 + 16)
                    load_xres(i * 2 + 2, 0)
                    sp.wait_ge(ts_full, i * 6 + 9)
                    load_xnext(i * 2 + 3)

            sp.dma_start(xnext[:, :, :], xrows(0, 0)).then_inc(xnext_in, 16)
            load_w(0, 0, 0, 0)
            sp.dma_start(lnab[:, :, :], lnab_in).then_inc(vec_in_sem, 16)
            sp.dma_start(vec[:, :, :], vec_in).then_inc(vec_in_sem, 16)
            load_w(0, 0, 1, 0)
            load_adj(0, 0)
            load_xres(0, 0)
            sp.wait_ge(ts_full, 3)
            load_xnext(1)
            load_adj(1, 1)
            load_xres(1, 1)
            round_of_loads(0, False)
            with sp.Fori(1, ROUNDS - 1) as i:
                round_of_loads(i, False)
            round_of_loads(ROUNDS - 1, True)
            sp.wait_ge(out_ready[1], ROUNDS)
            store(B - 1, 1)
            for x in range(2):
                sp.wait_ge(out_done[x], 16 * ROUNDS)

        @block.gpsimd
        def _(pool):
            def linked(ins, n):
                ins.then_inc(pool_chain, 1)
                pool.wait_ge(pool_chain, n)

            pool.memset(ones, 1.0).then_inc(pool_chain, 1)
            linked(pool.memset(ident[:, :], 0.0), 2)
            for dst, src, op, fill, cm, st in ((ident, ident[:, :], ALU.not_equal, 1.0, 1, -1),
                                               (low, ones, ALU.is_ge, 0.0, 1, -1),
                                               (below, ones, ALU.is_gt, 0.0, 1, -1),
                                               (above, ones, ALU.is_gt, 0.0, -1, 1)):
                pool.affine_select(out=dst[:, :], in_=src, compare_op=op, fill=fill, base=0,
                                   pattern=[[st, P]], channel_multiplier=cm).then_inc(const_done, 1)
            for x in range(2):
                pool.memset(hl_hi[x][:, :, H:VW].bitcast(F32), 1.0).then_inc(const_done, 1)
                pool.memset(hl_lo[x][:, :, H:VW].bitcast(F32), 0.0).then_inc(const_done, 1)
            pool.memset(hr_hi[1][:, :, H:VW].bitcast(F32), 1.0).then_inc(const_done, 1)
            pool.memset(hr_lo[1][:, :, H:VW].bitcast(F32), 0.0).then_inc(const_done, 1)

            def split_w(i, s, slot):
                n = w_index(i, s, slot)
                pool.wait_ge(w_split_hi, n + 1)
                pool.tensor_tensor(w_lo[:, slot, :, :], w_stage[:, :, :], w_hi[:, slot, :, :].bitcast(F32),
                                   ALU.subtract).then_inc(w_split_lo, 1)

            def values_lo(i, s, first, hi, lo):
                for k in range(NB):
                    n = HL_BEFORE[s] + first + k
                    pool.wait_ge(proj_hi, i * 56 + (PHI_BEFORE[s] + (6 if s < 4 else 0) + first + k + 1))
                    pool.tensor_tensor(lo[:, k, 0:H], pt[:, n % 2, 0:H], hi[:, k, 0:H].bitcast(F32),
                                       ALU.subtract).then_inc(val_lo, 1)

            def weights_lo(i, s, J):
                pool.wait_ge(weight_hi, step_count(i, s, 4, J))
                w = S if s < 4 else DW
                pool.tensor_tensor(d_lo[:, J, 0:w], td[:, J % 3, 0:w], d_hi[:, J, 0:w].bitcast(F32),
                                   ALU.subtract).then_inc(weight_lo, 1)

            def sum_exp(i, s, J):
                pool.wait_ge(exp_done, step_count(i, s, 4, J))
                if J == 1:
                    if s == 5:
                        pool.wait_ge(ring_full, job(i, 5, "z"))
                    elif late(i, 0):
                        pool.wait_ge(ring_full, job(i, 0, "z"))
                    pool.tensor_tensor(esum[:, :], td[:, 0, 0:S], td[:, 1, 0:S], ALU.add).then_inc(esum_done, 2)
                else:
                    pool.wait_ge(esum_done, i * 8 + ((s - 4) * 4 + J))
                    pool.tensor_tensor(esum[:, :], esum[:, :], td[:, J % 3, 0:S], ALU.add).then_inc(esum_done, 1)

            def round_of_pool(i):
                for s in range(STEPS):
                    x = s % 2
                    if s < 4:
                        if x == 0:
                            split_w(i, s, 2)
                        else:
                            split_w(i, s + 1, 0)
                        values_lo(i, s, 0, hl_hi[x], hl_lo[x])
                        if x == 1:
                            split_w(i, s + 1, 1)
                        for J in range(NB):
                            weights_lo(i, s, J)
                    else:
                        if x == 0:
                            split_w(i, s, 2)
                        values_lo(i, s, 0, hl_hi[x], hl_lo[x])
                        if x == 1:
                            split_w(i, s + 1, 0)
                        values_lo(i, s, 4, hr_hi[x], hr_lo[x])
                        sum_exp(i, s, 1)
                        weights_lo(i, s, 0)
                        sum_exp(i, s, 2)
                        weights_lo(i, s, 1)
                        sum_exp(i, s, 3)
                        weights_lo(i, s, 2)
                        weights_lo(i, s, 3)
                        if x == 1:
                            split_w(i, s + 1, 1)

            split_w(0, 0, 0)
            split_w(0, 0, 1)
            round_of_pool(0)
            with pool.Fori(1, ROUNDS) as i:
                round_of_pool(i)

        @block.scalar
        def _(act):
            def split_w(i, s, slot):
                n = w_index(i, s, slot)
                act.wait_ge(w_raw, n * 16 + 16)
                if not (isinstance(i, int) and i == 0 and s == 0):
                    q = s - 1
                    if q >= 0:
                        last = [("ml", 2), ("mr", 2), ("hl", 3)] if q < 4 else [("hl", 3), ("hr", 3), ("hs", 3)]
                        act.wait_ge(ring_full, job(i, q, *last[slot]))
                    else:
                        act.wait_ge(ring_full, i * JOBS_PER_ROUND)
                act.activation(w_hi[:, slot, :, :], w_stage[:, :, :], ACT.Copy).then_inc(w_split_hi, 1)

            def feature_hi(g_i, g_s, k):
                if g_s in (2, 3):
                    act.wait_ge(ht_pre, g_i * 6 + ((g_s - 2) * 3 + k + 1))
                    wait_ht_free(act, g_i, g_s, k)
                    src = pt[:, k % 2, :]
                    act.activation(ht_hi[:, k, :], src, ACT.Relu).then_inc(ht_hi_done, 1)
                    return
                if g_s in (0, 5):
                    act.wait_ge(ts_full, g_i * 6 + ((3 if g_s == 5 else 0) + k + 1))
                    src = score[k]
                else:
                    q = g_s - 1
                    act.wait_ge(ring_full, job(g_i, q, "t", k))
                    src = bank(q, "t", k)
                wait_ht_free(act, g_i, g_s, k)
                act.activation(ht_hi[:, k, :], src[:, :], ACT.Relu).then_inc(ht_hi_done, 1)

            def mixed_hi(i, s):
                for name, hi in (("ml", ml_hi), ("mr", mr_hi)):
                    for k in range(NC):
                        act.wait_ge(ring_full, job(i, s, name, k))
                        act.activation(hi[:, k, :], bank(s, name, k)[:, :], ACT.Copy).then_inc(proj_hi, 1)

            def values_hi(i, s, name, first, hi):
                for k in range(NB):
                    n = HL_BEFORE[s] + first + k
                    act.wait_ge(ring_free, freed(i, s, name, k))
                    act.activation(hi[:, k, 0:H], pt[:, n % 2, 0:H], ACT.Copy).then_inc(proj_hi, 1)

            def exp_of(i, s, J):
                if s < 4:
                    act.wait_ge(masked, i * 16 + (s * 4 + J + 1))
                    act.activation(td[:, J % 3, 0:S], td[:, J % 3, 0:S], ACT.Exp).then_inc(exp_done, 1)
                else:
                    act.wait_ge(max_added, i * 8 + ((s - 4) * 4 + J + 1))
                    if J == 3:
                        act.wait_ge(weight_lo, step_count(i, s, 4, 0))
                    elif J == 0:
                        act.wait_ge(weight_lo, i * 24 + 4 * s)
                    act.activation(td[:, J % 3, 0:S], score[J][:, :], ACT.Exp, scale=ROOT_H).then_inc(exp_done, 1)

            def weight_hi_of(i, s, J):
                act.wait_ge(weight_done, step_count(i, s, 4, J))
                w = S if s < 4 else DW
                act.activation(d_hi[:, J, 0:w], td[:, J % 3, 0:w], ACT.Copy).then_inc(weight_hi, 1)

            def round_of_act(i):
                for s in range(STEPS):
                    x = s % 2
                    g_i, g_s = (i, s + 1) if s < 5 else (i + 1, 0)
                    if s < 4:
                        mixed_hi(i, s)
                        if x == 0:
                            split_w(i, s, 2)
                        else:
                            split_w(i, s + 1, 0)
                        values_hi(i, s, "hl", 0, hl_hi[x])
                        if x == 1:
                            split_w(i, s + 1, 1)
                        exp_of(i, s, 0)
                        exp_of(i, s, 1)
                        weight_hi_of(i, s, 0)
                        weight_hi_of(i, s, 1)
                        for k in range(NC):
                            feature_hi(g_i, g_s, k)
                        exp_of(i, s, 2)
                        exp_of(i, s, 3)
                        weight_hi_of(i, s, 2)
                        weight_hi_of(i, s, 3)
                    else:
                        if x == 0:
                            split_w(i, s, 2)
                        values_hi(i, s, "hl", 0, hl_hi[x])
                        if x == 1:
                            split_w(i, s + 1, 0)
                        values_hi(i, s, "hr", 4, hr_hi[x])
                        exp_of(i, s, 0)
                        exp_of(i, s, 1)
                        exp_of(i, s, 2)
                        weight_hi_of(i, s, 0)
                        exp_of(i, s, 3)
                        weight_hi_of(i, s, 1)
                        weight_hi_of(i, s, 2)
                        for k in range(NC):
                            feature_hi(g_i, g_s, k)
                        weight_hi_of(i, s, 3)
                        if x == 1:
                            split_w(i, s + 1, 1)

            split_w(0, 0, 0)
            for k in range(NC):
                feature_hi(0, 0, k)
            split_w(0, 0, 1)
            round_of_act(0)
            with act.Fori(1, ROUNDS) as i:
                round_of_act(i)

        @block.tensor
        def _(pe):
            def mm3(dst, a, b, start, stop):
                pe.matmul(dst, a[0], b[0], start=start, stop=False)
                pe.matmul(dst, a[0], b[1], start=False, stop=False)
                return pe.matmul(dst, a[1], b[0], start=False, stop=stop)

            def feat(k, lo, hi):
                return ht_hi[:, k, lo:hi], ht_lo[:, k, lo:hi]

            def weight(slot, k, lo=0, hi=H):
                return w_hi[:, slot, k, lo:hi], w_lo[:, slot, k, lo:hi]

            def wait_bank(i, s, name, k=0):
                n = JOBS[s, name, k]
                if left_out(i) and n - 4 < left_out(i):
                    pe.wait_ge(ring_free, ROUNDS * len(FREES))
                    return
                if n < 4:
                    if isinstance(i, int) and i == 0:
                        return
                    before = max(m for m in range(JOBS_PER_ROUND - 4, JOBS_PER_ROUND) if m % 4 == n)
                    pe.wait_ge(ring_free, freed(i, *JOB_AT[before]) - len(FREES))
                    return
                q, what, c = JOB_AT[n - 4]
                if what == "t":
                    pe.wait_ge(ht_lo_done, step_count(i, q + 1, 3, c))
                else:
                    pe.wait_ge(ring_free, freed(i, q, what, c))

            def wait_feat(i, s, k):
                pe.wait_ge(ht_hi_done, step_count(i, s, 3, k))
                pe.wait_ge(ht_lo_done, step_count(i, s, 3, k))

            def wait_weight(i, s, slot):
                pe.wait_ge(w_split_lo, w_index(i, s, slot) + 1)

            def mix_keys(i, s, name, slot, outer):
                wait_weight(i, s, slot)
                if outer:
                    for k in range(NC):
                        wait_feat(i, s, k)
                        for c in range(NC):
                            if k == 0:
                                wait_bank(i, s, name, c)
                            m = mm3(bank(s, name, c)[:, :], weight(slot, k, c * P, (c + 1) * P), feat(k, 0, S),
                                    k == 0, k == NC - 1)
                            if k == NC - 1:
                                m.then_inc(ring_full, 1)
                    return
                for c in range(NC):
                    wait_bank(i, s, name, c)
                    for k in range(NC):
                        m = mm3(bank(s, name, c)[:, :], weight(slot, k, c * P, (c + 1) * P), feat(k, 0, S),
                                k == 0, k == NC - 1)
                    m.then_inc(ring_full, 1 if late(i, s) or c < NC - 1 else 1 + 1 + NB)

            def values(i, s, name, slot):
                wait_weight(i, s, slot)
                for b in range(NB):
                    wait_bank(i, s, name, b)
                    for k in range(NC):
                        m = mm3(bank(s, name, b)[:, 0:H], feat(k, b * P, (b + 1) * P), weight(slot, k),
                                k == 0, k == NC - 1)
                    m.then_inc(ring_full, 1)

            def values_outer(i, s, name, slot, ks, free_feat):
                for k in ks:
                    if k == 0:
                        wait_weight(i, s, slot)
                    if not free_feat:
                        wait_feat(i, s, k)
                    for b in range(NB):
                        if k == 0:
                            wait_bank(i, s, name, b)
                        m = mm3(bank(s, name, b)[:, 0:H], feat(k, b * P, (b + 1) * P), weight(slot, k),
                                k == 0, k == NC - 1)
                        if k == NC - 1:
                            m.then_inc(ring_full, 1)
                    if free_feat and k < NC - 1:
                        m.then_inc(ht_free, 1)

            def exp_sums(i, s):
                wait_bank(i, s, "z")
                pe.wait_ge(esum_done, (i * 8 + 4) if s == 5 else i * 8)
                for b in range(NB):
                    m = pe.matmul(bank(s, "z")[:, b:b + 1], esum[:, b * P:(b + 1) * P], ones[:, 0:1],
                                  start=True, stop=True)
                m.then_inc(ring_full, 1)

            def context(i, s):
                q = (s - 1) % STEPS
                x = q % 2
                qi = i if s else i - 1
                values_before = (qi * 32) + HL_BEFORE[q] + (4 if q < 4 else 8)
                pe.wait_ge(val_lo, values_before)
                for b in range(NB):
                    wait_bank(i, s, "c", b)
                    terms = []
                    for J in range(NB):
                        cols = slice(b * P, (b + 1) * P)
                        if q < 4 or J > b:
                            terms.append((J, cols, hl_hi[x], hl_lo[x]))
                        elif J == b:
                            terms.append((J, cols, hl_hi[x], hl_lo[x]))
                            terms.append((J, slice(S, DW), hr_hi[x], hr_lo[x]))
                        else:
                            terms.append((J, cols, hr_hi[x], hr_lo[x]))
                    for n, (J, cols, vh, vl) in enumerate(terms):
                        if b == 0:
                            pe.wait_ge(weight_lo, step_count(qi, q, 4, J))
                        m = mm3(bank(s, "c", b)[:, 0:VW], (d_hi[:, J, cols], d_lo[:, J, cols]),
                                (vh[:, J, :], vl[:, J, :]), n == 0, n == len(terms) - 1)
                    m.then_inc(ring_full, 1)

            def transposes(i, s, k, dst, full):
                src = xnext if s in (5, 0, -1) else xhat
                if k == 0:
                    pe.wait_ge(xhat_ready, step_count(i, s, 1) + 1)
                for b in range(NB):
                    m = pe.transpose(dst[:, b * P:(b + 1) * P], src[:, b, k * P:(k + 1) * P], ident[:, :])
                m.then_inc(full, 1)

            def edge_scores(i, s, J, ks, free):
                left, right = score[2 * (J % 2)], score[2 * (J % 2) + 1]
                lw = max(MIN_N, (J + 1) * P)
                rl = min(S - MIN_N, J * P)
                for k in ks:
                    mm3(left[:, 0:lw], (ml_hi[:, k, J * P:(J + 1) * P], ml_lo[:, k, J * P:(J + 1) * P]),
                        feat(k, 0, lw), k == 0, k == NC - 1)
                    m = mm3(right[:, rl:S], (mr_hi[:, k, J * P:(J + 1) * P], mr_lo[:, k, J * P:(J + 1) * P]),
                            feat(k, rl, S), k == 0, k == NC - 1)
                    if k == NC - 1:
                        m.then_inc(score_full, 1)
                    elif free:
                        m.then_inc(ht_free, 1)

            def edge_step(i, s):
                mix_keys(i, s, "ml", 0, True)
                mix_keys(i, s, "mr", 1, False)
                if late(i, s):
                    if s == 0:
                        exp_sums(i, s)
                    context(i, s)
                values(i, s, "hl", 2)
                pe.wait_ge(ring_free, freed(i, s, "mr", 2))
                if s > 0:
                    pe.wait_ge(masked, i * 16 + 4 * s)
                else:
                    if late(i, s):
                        pe.wait_ge(exp_done, i * 24)
                    pe.wait_ge(ht_lo_done, i * 18 + 3)
                edge_scores(i, s, 0, range(NC), False)
                edge_scores(i, s, 1, range(NC), False)
                for k in range(NC):
                    if k == 0:
                        pe.wait_ge(masked, i * 16 + (4 * s + 1))
                    edge_scores(i, s, 2, [k], False)
                    if k == 0:
                        pe.wait_ge(masked, i * 16 + (4 * s + 2))
                    edge_scores(i, s, 3, [k], True)
                    if k == 0:
                        for c in range(NC):
                            if s == 3 or True:
                                wait_bank(i, s, "t", c)
                            transposes(i, s, c, bank(s, "t", c), ring_full)

            def soft_step(i, s):
                values_outer(i, s, "hl", 0, range(NC), False)
                if s == 5:
                    exp_sums(i, s)
                context(i, s)
                if s == 4:
                    pe.wait_ge(masked, i * 16 + 16)
                else:
                    pe.wait_ge(exp_done, i * 24 + 20)
                    pe.wait_ge(ht_lo_done, i * 18 + 18 - 0)
                for J in range(NB):
                    for k in range(NC):
                        m = mm3(score[J][:, :], feat(k, J * P, (J + 1) * P), feat(k, 0, S), k == 0, k == NC - 1)
                    m.then_inc(score_full, 1)
                values(i, s, "hr", 1)
                pe.wait_ge(max_ready, i * 2 + (s - 3))
                for J in range(NB):
                    pe.matmul(score[J][:, :], ones_r[:, :], negmax[:, :, :].rearrange("p b q -> p (b q)"),
                              start=False, stop=True, skip_group_check=True).then_inc(max_added, 1)
                values_outer(i, s, "hs", 2, range(NC - 1), True)
                for c in range(NC):
                    pe.wait_ge(exp_done, step_count(i, s, 4, c))
                    transposes(i, s, c, score[c], ts_full)
                values_outer(i, s, "hs", 2, [NC - 1], True)

            def round_of_pe(i):
                for s in range(4):
                    edge_step(i, s)
                for s in range(4, STEPS):
                    soft_step(i, s)

            pe.wait_ge(const_done, 10)
            for c in range(NC):
                transposes(0, -1, c, score[c], ts_full)
            round_of_pe(0)
            with pe.Fori(1, ROUNDS) as i:
                round_of_pe(i)
            exp_sums(ROUNDS, 0)
            context(ROUNDS, 0)

        @block.vector
        def _(dve):
            chain = {"base": 0, "n": 0}

            def link(ins):
                ins.then_inc(dve_chain, 1)
                chain["n"] += 1
                dve.wait_ge(dve_chain, chain["base"] + chain["n"])

            def rsqrt():
                link(dve.tensor_scalar(nt.bitcast(I32), var.bitcast(I32), 1, None, ALU.logical_shift_right))
                link(dve.tensor_scalar(rs.bitcast(I32), nt.bitcast(I32), -1.0, NEG_HALF_MAGIC, ALU.mult, ALU.add))
                for _ in range(4):
                    link(dve.tensor_tensor(nt, rs, rs, ALU.mult))
                    link(dve.scalar_tensor_tensor(nt, nt, -0.5, var, ALU.mult, ALU.mult))
                    link(dve.scalar_tensor_tensor(rs, nt, 1.5, rs, ALU.add, ALU.mult))

            def row_moments():
                mean_e, mean_o, ssd_e, ssd_o = (stats[:, :, q] for q in (1, 4, 2, 5))
                dve.tensor_tensor(msum, mean_e, mean_o, ALU.add).then_inc(dve_chain, 1)
                dve.tensor_tensor(nt, mean_e, mean_o, ALU.subtract).then_inc(dve_chain, 1)
                chain["n"] += 2
                link(dve.tensor_tensor(var, ssd_e, ssd_o, ALU.add))
                link(dve.scalar_tensor_tensor(nt, nt, 0.25, nt, ALU.mult, ALU.mult))
                link(dve.scalar_tensor_tensor(var, var, 1.0 / H, nt, ALU.mult, ALU.add))

            def normalise(src, dst, publish):
                link(dve.scalar_tensor_tensor(nb, msum, -0.5, rs, ALU.mult, ALU.mult))
                for b in range(NB):
                    ins = dve.tensor_scalar(dst[:, b, :], src[:, b, :], rs[:, b:b + 1], nb[:, b:b + 1],
                                            ALU.mult, ALU.add)
                    if b == NB - 1:
                        if publish:
                            ins.then_inc(xhat_ready, 1)
                        else:
                            link(ins)

            def pre_norm(src, dst, eps):
                row_moments()
                link(dve.tensor_scalar(var, var, eps, None, ALU.add))
                rsqrt()
                normalise(src, dst, True)

            def load_norm(n):
                dve.wait_ge(xnext_in, n)
                for b in range(NB):
                    link(dve.bn_stats(stats[:, b, :], xnext[:, b, :]))
                pre_norm(xnext, xnext, 1e-5)

            def scale_shift(dst, scale, shift):
                for b in range(NB):
                    link(dve.tensor_tensor(dst[:, b, :], dst[:, b, :], vec[:, scale, :], ALU.mult))
                    link(dve.tensor_tensor(dst[:, b, :], dst[:, b, :], vec[:, shift, :], ALU.add))

            def edge_context(i, s):
                q = (s - 1) % STEPS
                x = q % 2
                for b in range(NB):
                    src = bank(s, "c", b)
                    dve.wait_ge(ring_full, job(i, s, "c", b))
                    link(dve.tensor_scalar(den[:, b:b + 1], src[:, H:H + 1], 1e-10, None, ALU.add))
                    link(dve.reciprocal(rden[:, b:b + 1], den[:, b:b + 1]))
                    dve.tensor_scalar(xhat[:, b, :], src[:, 0:H], rden[:, b:b + 1], None, ALU.mult).then_inc(ring_free, 1)
                    dve.wait_ge(ring_free, freed(i, s, "c", b))
                    link(dve.bn_stats(stats[:, b, :], xhat[:, b, :]))
                row_moments()
                link(dve.tensor_scalar(var, var, H / (H - 1.0), 1e-30, ALU.mult, ALU.max))
                rsqrt()
                link(dve.tensor_tensor(nt, var, rs, ALU.mult))
                link(dve.tensor_scalar(nt, nt, 1e-3, None, ALU.add))
                link(dve.reciprocal(rs, nt))
                if q < 2:
                    normalise(xhat, xhat, True)
                    return
                normalise(xhat, xhat, False)
                scale_shift(xhat, 2, 3)
                dve.wait_ge(xres_in[x], i * 16 + 16)
                for b in range(NB):
                    link(dve.scalar_tensor_tensor(xres[x][:, b, :], xhat[:, b, :], 0.0, xres[x][:, b, :],
                                                  ALU.max, ALU.add))
                    link(dve.bn_stats(stats[:, b, :], xres[x][:, b, :]))
                pre_norm(xres[x], xhat, 1e-5)

            def soft_context(i, s):
                q = (s - 1) % STEPS
                x = q % 2
                dd = diag[:, x, :]
                dve.wait_ge(ring_full, job(i, s, "z"))
                dve.tensor_copy(zc, bank(s, "z")[:, 0:NB]).then_inc(ring_free, 1)
                dve.wait_ge(ring_free, freed(i, s, "z"))
                for b in range(NB):
                    src = bank(s, "c", b)
                    c = slice(b, b + 1)
                    dve.wait_ge(ring_full, job(i, s, "c", b))
                    link(dve.scalar_tensor_tensor(den[:, c], zc[:, c], 1e-10, src[:, H:H + 1], ALU.mult, ALU.add))
                    link(dve.tensor_tensor(den[:, c], den[:, c], dd[:, c], ALU.add))
                    link(dve.reciprocal(rden[:, c], den[:, c]))
                    link(dve.tensor_tensor(ddr[:, c], dd[:, c], rden[:, c], ALU.mult))
                    dve.tensor_scalar(xhat[:, b, :], src[:, 0:H], rden[:, c], None, ALU.mult).then_inc(ring_free, 1)
                    dve.wait_ge(ring_free, freed(i, s, "c", b))
                    link(dve.scalar_tensor_tensor(xhat[:, b, :], hs[x][:, b, :], ddr[:, c], xhat[:, b, :],
                                                  ALU.mult, ALU.add))
                    link(dve.bn_stats(stats[:, b, :], xhat[:, b, :]))
                row_moments()
                link(dve.tensor_scalar(var, var, 1e-12, None, ALU.add))
                rsqrt()
                normalise(xhat, xhat, False)
                scale_shift(xhat, 7, 8)
                for b in range(NB):
                    ins = dve.scalar_tensor_tensor(xres[x][:, b, :], xhat[:, b, :], 0.0, xres[x][:, b, :],
                                                   ALU.max, ALU.add)
                    if b == NB - 1:
                        ins.then_inc(out_ready[x], 1)
                    else:
                        link(ins)

            def feature_lo(g_i, g_s, k):
                in_ring = g_s not in (0, 5)
                src = bank(g_s - 1, "t", k) if in_ring else score[k]
                if g_s in (2, 3):
                    dve.wait_ge(ring_full, job(g_i, g_s - 1, "t", k))
                    if k < 2:
                        dve.wait_ge(val_lo, g_i * 32 + (HL_BEFORE[g_s]))
                    else:
                        dve.wait_ge(ht_lo_done, step_count(g_i, g_s, 3, 0))
                    dve.tensor_scalar(pt[:, k % 2, :], src[:, :], lnab[:, 0, k:k + 1], lnab[:, 1, k:k + 1],
                                      ALU.mult, ALU.add).then_inc(ht_pre, 1)
                    dve.wait_ge(ht_hi_done, step_count(g_i, g_s, 3, k))
                    ins = dve.scalar_tensor_tensor(ht_lo[:, k, :], pt[:, k % 2, :], 0.0,
                                                   ht_hi[:, k, :].bitcast(F32), ALU.max, ALU.subtract)
                else:
                    dve.wait_ge(ht_hi_done, step_count(g_i, g_s, 3, k))
                    ins = dve.scalar_tensor_tensor(ht_lo[:, k, :], src[:, :], 0.0,
                                                   ht_hi[:, k, :].bitcast(F32), ALU.max, ALU.subtract)
                ins.then_inc(ht_lo_done, 1)

            def mixed_lo(i, s):
                for first, name, hi, lo in ((0, "ml", ml_hi, ml_lo), (NC, "mr", mr_hi, mr_lo)):
                    for k in range(NC):
                        dve.wait_ge(proj_hi, i * 56 + (PHI_BEFORE[s] + first + k + 1))
                        skipped = 0 if late(i, s) or name == "ml" or k < NC - 1 else 1 + NB
                        dve.tensor_tensor(lo[:, k, :], bank(s, name, k)[:, :], hi[:, k, :].bitcast(F32),
                                          ALU.subtract).then_inc(ring_free, 1 + skipped)

            def values_bias(i, s, name, first, bias):
                for k in range(NB):
                    n = HL_BEFORE[s] + first + k
                    dve.wait_ge(ring_full, job(i, s, name, k))
                    if not (isinstance(i, int) and i == 0 and n < 2):
                        dve.wait_ge(val_lo, i * 32 + (n - 1))
                    dve.tensor_tensor(pt[:, n % 2, 0:H], bank(s, name, k)[:, 0:H], vec[:, bias, :],
                                      ALU.add).then_inc(ring_free, 1)

            def mask_of(i, s, J):
                x = s % 2
                left, right = score[2 * (J % 2)], score[2 * (J % 2) + 1]
                lo, hi = J * P, (J + 1) * P
                t = td[:, J % 3, :]
                dve.wait_ge(score_full, step_count(i, s, 4, J))
                if J == 0 and not (isinstance(i, int) and i == 0 and s == 0):
                    dve.wait_ge(weight_lo, i * 24 + 4 * s)
                elif J == 3:
                    dve.wait_ge(weight_lo, step_count(i, s, 4, 0))
                if J > 0:
                    dve.scalar_tensor_tensor(t[:, 0:lo], left[:, 0:lo], ROOT_H, adjt[x][:, J, 0:lo], ALU.mult, ALU.mult)
                    rest = slice(lo, S)
                else:
                    dve.scalar_tensor_tensor(t[:, P:S], right[:, P:S], ROOT_H, adjn[x][:, P:S], ALU.mult, ALU.mult)
                    rest = slice(0, P)
                link(dve.copy_predicated(right[:, lo:hi], low[:, :].bitcast(I32), left[:, lo:hi]))
                dve.scalar_tensor_tensor(t[:, rest], right[:, rest], ROOT_H,
                                         adjn[x][:, AT[J]:AT[J] + rest.stop - rest.start],
                                         ALU.mult, ALU.mult).then_inc(masked, 1)

            def weight_of(i, s, J):
                x = s % 2
                t = td[:, J % 3, :]
                dve.wait_ge(exp_done, step_count(i, s, 4, J))
                if s < 4:
                    dve.tensor_tensor(t[:, 0:S], t[:, 0:S], adjt[x][:, J, :], ALU.mult).then_inc(weight_done, 1)
                    return
                lo, hi = J * P, (J + 1) * P
                dve.wait_ge(esum_done, i * 8 + ((s - 4) * 4 + J + 1))
                link(dve.tensor_tensor(t[:, 0:S], t[:, 0:S], adjt[x][:, J, :], ALU.mult))
                link(dve.scalar_tensor_tensor(t[:, S:DW], t[:, lo:hi], 1.0, ident[:, :], ALU.mult, ALU.mult,
                                              accum_out=diag[:, x, J:J + 1]))
                link(dve.tensor_tensor(t[:, S:DW], t[:, lo:hi], above[:, :], ALU.mult))
                dve.tensor_tensor(t[:, lo:hi], t[:, lo:hi], below[:, :], ALU.mult).then_inc(weight_done, 1)

            def maxima(i, s):
                for J in range(NB):
                    dve.wait_ge(score_full, step_count(i, s, 4, J))
                    link(dve.tensor_reduce(mx[:, J:J + 1], score[J][:, :], AX_X, ALU.max))
                if s == 5:
                    dve.wait_ge(max_added, i * 8 + 4)
                elif late(i, 0):
                    dve.wait_ge(max_added, i * 8)
                for J in range(NB):
                    ins = dve.tensor_scalar(negmax[:, J, :], ident[:, :], mx[:, J:J + 1], -1.0, ALU.mult, ALU.mult)
                    if J == NB - 1:
                        ins.then_inc(max_ready, 1)
                    else:
                        link(ins)

            def mirror_adj(i, x):
                for J in range(NB):
                    ins = dve.copy_predicated(adjn[x][:, AT[J]:AT[J] + P], low[:, :].bitcast(I32),
                                              adjt[x][:, J, J * P:(J + 1) * P])
                link(ins)

            def round_of_dve(i):
                for s in range(STEPS):
                    x = s % 2
                    g_i, g_s = (i, s + 1) if s < 5 else (i + 1, 0)
                    if s < 4:
                        if s < 2:
                            dve.wait_ge(adj_in_sem[x], i * 80 + 80)
                        mixed_lo(i, s)
                        if s == 0:
                            load_norm(i * 32 + 32)
                            if late(i, s):
                                soft_context(i, s)
                        else:
                            edge_context(i, s)
                        values_bias(i, s, "hl", 0, s // 2)
                        if s < 2:
                            mirror_adj(i, x)
                        mask_of(i, s, 0)
                        mask_of(i, s, 1)
                        weight_of(i, s, 0)
                        weight_of(i, s, 1)
                        for k in range(NC):
                            feature_lo(g_i, g_s, k)
                        mask_of(i, s, 2)
                        mask_of(i, s, 3)
                        weight_of(i, s, 2)
                        weight_of(i, s, 3)
                    else:
                        values_bias(i, s, "hl", 0, 4)
                        if s == 4:
                            edge_context(i, s)
                        else:
                            soft_context(i, s)
                        maxima(i, s)
                        dve.wait_ge(ring_full, job(i, s, "hr", 0))
                        if s == 4:
                            link(dve.memset(hr_hi[0][:, :, H:VW].bitcast(F32), 1.0))
                            link(dve.memset(hr_lo[0][:, :, H:VW].bitcast(F32), 0.0))
                        values_bias(i, s, "hr", 4, 5)
                        if s == 5:
                            load_norm(i * 32 + 48)
                        for J in range(NB):
                            weight_of(i, s, J)
                        for k in range(NC):
                            feature_lo(g_i, g_s, k)
                        for b in range(NB):
                            dve.wait_ge(ring_full, job(i, s, "hs", b))
                            dve.tensor_tensor(hs[x][:, b, :], bank(s, "hs", b)[:, 0:H], vec[:, 6, :],
                                              ALU.add).then_inc(ring_free, 1)

            dve.wait_ge(const_done, 10)
            load_norm(16)
            for k in range(NC):
                feature_lo(0, 0, k)
            dve.wait_ge(vec_in_sem, 32)
            round_of_dve(0)
            after_first = chain["n"]
            chain["n"] = 0
            per_round = DVE_LINKS
            with dve.Fori(1, ROUNDS) as i:
                chain["base"] = i * per_round + (after_first - per_round)
                round_of_dve(i)
            assert chain["n"] == per_round, chain["n"]
            chain["base"] = after_first + (ROUNDS - 1) * per_round
            chain["n"] = 0
            soft_context(ROUNDS, 0)


DVE_LINKS = 442


def kernel(x, adj, L0_gnn_W_left, L0_gnn_W_right, L0_gnn_W_lin, L0_gnn_b_lin, L0_gnn_ln_a, L0_gnn_ln_b,
           L1_gnn_W_left, L1_gnn_b_left, L1_gnn_W_self, L1_gnn_b_self, L1_gnn_W_right, L1_gnn_b_right,
           L1_gnn_gamma, L1_gnn_beta):
    import numpy as np
    import concourse.bacc as bacc
    from concourse.bass_utils import run_bass_kernel_spmd

    f = np.ascontiguousarray
    w = f(np.stack([np.swapaxes(np.asarray(m), 0, 1) for m in (
        L0_gnn_W_left[0], L0_gnn_W_right[0], L0_gnn_W_lin[0],
        L0_gnn_W_left[1], L0_gnn_W_right[1], L0_gnn_W_lin[1],
        L1_gnn_W_left, L1_gnn_W_right, L1_gnn_W_self)]).reshape(3, 3, H, H))
    vec = np.stack([np.asarray(v) for v in (
        L0_gnn_b_lin[0], L0_gnn_b_lin[1], L0_gnn_ln_a[1], L0_gnn_ln_b[1],
        L1_gnn_b_left, L1_gnn_b_right, L1_gnn_b_self, L1_gnn_gamma, L1_gnn_beta)])
    vec = f(np.broadcast_to(vec[None], (P, 9, H)))
    lnab = f(np.stack([np.asarray(L0_gnn_ln_a[0]).reshape(NC, P),
                       np.asarray(L0_gnn_ln_b[0]).reshape(NC, P)]).transpose(2, 0, 1))
    arrays = {"x": f(x), "adj": f(adj), "adjt": f(np.swapaxes(np.asarray(adj), 1, 2)), "w": w, "vec": vec,
              "lnab": lnab}
    nc = bacc.Bacc("TRN2", target_bir_lowering=False, num_devices=1)
    args = [nc.dram_tensor(f"in_{n}", a.shape, mybir.dt.from_np(a.dtype), kind="ExternalInput").ap()
            for n, a in arrays.items()]
    out = nc.dram_tensor("out", (B, S, H), F32, kind="ExternalOutput").ap()
    gnn_kernel(nc, *args, out)
    r = run_bass_kernel_spmd(nc, [{f"in_{n}": a for n, a in arrays.items()}], core_ids=[0])
    return r.results[0]["out"]
```

```python
from contextlib import ExitStack

import concourse.bass as bass
from concourse import mybir

F32 = mybir.dt.float32
F32R = mybir.dt.float32r
I32 = mybir.dt.int32
ALU = mybir.AluOpType
ACT = mybir.ActivationFunctionType
AX_X = mybir.AxisListType.X

P = 128
B, S, H = 16, 512, 384
NB = S // P
NC = H // P
VW = H + 2
DW = S + P
STEPS = 6
ROUNDS = B // 2
ROOT_H = float(H) ** -0.5
MIN_N = 256
NEG_HALF_MAGIC = float(0x5F3759DF)


def job_table():
    table, frees, n = {}, {}, 0
    for s in range(STEPS):
        z = [("z", 1)] if s in (0, 5) else []
        if s < 4:
            order = [("ml", NC), ("mr", NC)] + z + [("c", NB), ("hl", NB), ("t", NC)]
        else:
            order = [("hl", NB)] + z + [("c", NB), ("hr", NB), ("hs", NB)]
        for name, count in order:
            for k in range(count):
                table[s, name, k] = n
                n += 1
                if name not in ("t", "c"):
                    frees[s, name, k] = len(frees)
    return table, n, frees


JOBS, JOBS_PER_ROUND, FREES = job_table()
JOB_AT = {n: key for key, n in JOBS.items()}
HL_BEFORE = [4 * s if s < 4 else 16 + 8 * (s - 4) for s in range(STEPS)]
PHI_BEFORE = [10 * s if s < 4 else 40 + 8 * (s - 4) for s in range(STEPS)]


def gnn_kernel(nc, x_in, adj_in, adjt_in, w_in, vec_in, lnab_in, out):
    with ExitStack() as ctx:
        def sb(name, shape, dt=F32):
            return ctx.enter_context(nc.sbuf_tensor(name, shape, dt))

        def sem(name):
            return ctx.enter_context(nc.semaphore(name))

        ring = [ctx.enter_context(nc.psum_tensor(f"ring{k}", [P, 512], F32)) for k in range(4)]
        score = [ctx.enter_context(nc.psum_tensor(f"score{k}", [P, 512], F32)) for k in range(4)]

        w_stage = sb("w_stage", [P, NC, H])
        w_hi = sb("w_hi", [P, 3, NC, H], F32R)
        w_lo = sb("w_lo", [P, 3, NC, H], F32R)
        vec = sb("vec", [P, 9, H])
        lnab = sb("lnab", [P, 2, NC])
        ht_hi = sb("ht_hi", [P, NC, S], F32R)
        ht_lo = sb("ht_lo", [P, NC, S], F32R)
        mix = sb("mix", [P, 4 * NC * S], F32R)
        ml_hi, ml_lo, mr_hi, mr_lo = (
            mix[:, q * NC * S:(q + 1) * NC * S].rearrange("p (c s) -> p c s", c=NC) for q in range(4))
        hl_hi = [sb(f"hl_hi{x}", [P, NB, VW], F32R) for x in range(2)]
        hl_lo = [sb(f"hl_lo{x}", [P, NB, VW], F32R) for x in range(2)]
        hrb = sb("hrb", [P, 2 * NB * VW], F32R)
        hr_hi, hr_lo = ([r[:, q * NB * VW:(q + 1) * NB * VW].rearrange("p (b v) -> p b v", b=NB)
                         for r in (mix, hrb)] for q in range(2))
        d_hi = sb("d_hi", [P, NB, DW], F32R)
        d_lo = sb("d_lo", [P, NB, DW], F32R)
        adjt = [sb(f"adjt{x}", [P, NB, S]) for x in range(2)]
        adjn = [sb(f"adjn{x}", [P, NB * H]) for x in range(2)]
        hs = [adjn[x][:, :].rearrange("p (b v) -> p b v", b=NB) for x in range(2)]
        AT = [sum(S - P * k for k in range(J)) for J in range(NB + 1)]
        xres = [sb(f"xres{x}", [P, NB, H]) for x in range(2)]
        xnext = sb("xnext", [P, NB, H])
        xhat = sb("xhat", [P, NB, H])
        td = sb("td", [P, 3, DW])
        esum = sb("esum", [P, S])
        pt = sb("pt", [P, 2, S])
        negmax = sb("negmax", [P, NB, P], F32R)
        ident = sb("ident", [P, P])
        low = sb("low", [P, P])
        below = sb("below", [P, P])
        above = sb("above", [P, P])
        ones_r = sb("ones_r", [P, P], F32R)
        ones = ones_r[:, :].bitcast(F32)
        stats = sb("stats", [P, NB, 6])
        small = sb("small", [P, 16, NB])
        den, rden, var, nt, mx, zc, ddr, msum = (small[:, k, :] for k in range(8))
        ctx_rs, ctx_nb, pre_rs, pre_nb = (small[:, k, :] for k in range(8, 12))
        diag = small[:, 12:14, :]

        const_done = sem("const_done")
        vec_in_sem = sem("vec_in_sem")
        w_raw = sem("w_raw")
        xnext_in = sem("xnext_in")
        xres_in = [sem(f"xres_in{x}") for x in range(2)]
        adj_in_sem = [sem(f"adj_in{x}") for x in range(2)]
        w_split_hi = sem("w_split_hi")
        w_split_lo = sem("w_split_lo")
        ring_full = sem("ring_full")
        ring_free = sem("ring_free")
        sums_ready = sem("sums_ready")
        context_free = sem("context_free")
        context_scaled = sem("context_scaled")
        normed = sem("normed")
        scaled = sem("scaled")
        shifted = sem("shifted")
        pre_scaled = sem("pre_scaled")
        xhat_ready = sem("xhat_ready")
        ht_pre = sem("ht_pre")
        ht_hi_done = sem("ht_hi_done")
        ht_lo_done = sem("ht_lo_done")
        ht_free = sem("ht_free")
        ts_full = sem("ts_full")
        proj_hi = sem("proj_hi")
        val_lo = sem("val_lo")
        score_full = sem("score_full")
        masked = sem("masked")
        exp_done = sem("exp_done")
        esum_done = sem("esum_done")
        weight_done = sem("weight_done")
        weight_hi = sem("weight_hi")
        weight_lo = sem("weight_lo")
        max_ready = sem("max_ready")
        max_added = sem("max_added")
        adjn_ready = sem("adjn_ready")
        out_ready = [sem(f"out_ready{x}") for x in range(2)]
        out_done = [sem(f"out_done{x}") for x in range(2)]
        dve_chain = sem("dve_chain")
        pool_chain = sem("pool_chain")

        def left_out(i):
            return 2 * NC if isinstance(i, int) and i == ROUNDS else 0

        def job(i, s, name, k=0):
            return i * JOBS_PER_ROUND + (JOBS[s, name, k] + 1 - left_out(i))

        def freed(i, s, name, k=0):
            return i * len(FREES) + (FREES[s, name, k] + 1 - left_out(i))

        def contexts_read(i, s, b):
            return i * (STEPS * NB) + (s * NB + b + 1 - NB)

        def finished(i, s, b):
            return i * (4 * NB) + ({0: 0, 3: NB, 4: 2 * NB, 5: 3 * NB}[s] + b + 1 - NB)

        def prenorms(i, s):
            return i * 4 + ({0: 0, 3: 1, 4: 2, 5: 3}[s] + 2)

        def bank(s, name, k=0):
            return ring[JOBS[s, name, k] % 4]

        def step_count(i, s, per, k=0):
            return i * (STEPS * per) + (s * per + k + 1)

        def late(i, s):
            return not (isinstance(i, int) and i == 0 and s == 0)

        def wait_ht_free(eng, g_i, g_s, k):
            if isinstance(g_i, int) and g_i == 0 and g_s == 0:
                return
            if k < NC - 1:
                eng.wait_ge(ht_free, g_i * (2 * STEPS) + (2 * g_s - 2 + k + 1))
            elif g_s == 0:
                eng.wait_ge(ring_full, g_i * JOBS_PER_ROUND)
            elif g_s == 5:
                eng.wait_ge(ring_full, job(g_i, 4, "hs", NB - 1))
            else:
                eng.wait_ge(score_full, step_count(g_i, g_s - 1, 4, 3))

        def w_index(i, s, slot):
            return i * 9 + (3 * (s // 2) + slot)

        def xrows(i, x):
            return x_in[bass.ds(i, 1), :, :].rearrange("a (b p) h -> p (a b) h", p=P)

        block = ctx.enter_context(nc.Block())

        @block.sync
        def _(sp):
            def load_w(i, s, slot, ahead):
                n = w_index(i, s, slot)
                if not (isinstance(n, int) and n == 0):
                    sp.wait_ge(w_split_lo, n)
                layer = (s // 2) % 3
                sp.dma_start(w_stage[:, :, :], w_in[layer, slot].rearrange("(c p) o -> p c o", p=P)).then_inc(w_raw, 16)

            def load_adj(b, x):
                sp.dma_start(adjt[x][:, :, :],
                             adjt_in[bass.ds(b, 1), :, :].rearrange("a (b p) s -> p (a b) s", p=P)).then_inc(adj_in_sem[x], 16)
                for J in range(NB):
                    sp.dma_start(adjn[x][:, AT[J]:AT[J + 1]],
                                 adj_in[bass.ds(b, 1), J * P:(J + 1) * P, J * P:S].rearrange("a p s -> (a p) s")
                                 ).then_inc(adj_in_sem[x], 16)

            def load_xnext(b):
                sp.dma_start(xnext[:, :, :], xrows(b, 0)).then_inc(xnext_in, 16)

            def load_xres(b, x):
                sp.dma_start(xres[x][:, :, :], xrows(b, x)).then_inc(xres_in[x], 16)

            def store(b, x):
                sp.dma_start(out[bass.ds(b, 1), :, :].rearrange("a (b p) h -> p (a b) h", p=P),
                             xres[x][:, :, :]).then_inc(out_done[x], 16)

            def round_of_loads(i, last):
                load_w(i, 0, 2, 0)
                if late(i, 0):
                    sp.wait_ge(out_ready[1], i)
                    store(i * 2 - 1, 1)
                    sp.wait_ge(weight_done, i * 24)
                    load_adj(i * 2 + 1, 1)
                    sp.wait_ge(out_done[1], i * 16)
                    load_xres(i * 2 + 1, 1)
                load_w(i, 2, 0, 0)
                load_w(i, 2, 1, 0)
                sp.wait_ge(ring_full, job(i, 0, "t", 2))
                load_xnext(0 if last else i * 2 + 2)
                load_w(i, 2, 2, 0)
                load_w(i, 4, 0, 0)
                load_w(i, 4, 1, 0)
                load_w(i, 4, 2, 0)
                load_w(i, 6, 0, 0)
                load_w(i, 6, 1, 0)
                sp.wait_ge(out_ready[0], i + 1)
                store(i * 2, 0)
                if not last:
                    sp.wait_ge(weight_done, i * 24 + 20)
                    load_adj(i * 2 + 2, 0)
                    sp.wait_ge(out_done[0], i * 16 + 16)
                    load_xres(i * 2 + 2, 0)
                    sp.wait_ge(ts_full, i * 6 + 9)
                    load_xnext(i * 2 + 3)

            sp.dma_start(xnext[:, :, :], xrows(0, 0)).then_inc(xnext_in, 16)
            load_w(0, 0, 0, 0)
            sp.dma_start(lnab[:, :, :], lnab_in).then_inc(vec_in_sem, 16)
            sp.dma_start(vec[:, :, :], vec_in).then_inc(vec_in_sem, 16)
            load_w(0, 0, 1, 0)
            load_adj(0, 0)
            load_xres(0, 0)
            sp.wait_ge(ts_full, 3)
            load_xnext(1)
            load_adj(1, 1)
            load_xres(1, 1)
            round_of_loads(0, False)
            with sp.Fori(1, ROUNDS - 1) as i:
                round_of_loads(i, False)
            round_of_loads(ROUNDS - 1, True)
            sp.wait_ge(out_ready[1], ROUNDS)
            store(B - 1, 1)
            for x in range(2):
                sp.wait_ge(out_done[x], 16 * ROUNDS)

        @block.gpsimd
        def _(pool):
            chain = {"base": 0, "n": 2}
            pool.memset(ones, 1.0).then_inc(pool_chain, 1)
            pool.memset(ident[:, :], 0.0).then_inc(pool_chain, 1)
            pool.wait_ge(pool_chain, 2)
            for dst, src, op, fill, cm, st in ((ident, ident[:, :], ALU.not_equal, 1.0, 1, -1),
                                               (low, ones, ALU.is_ge, 0.0, 1, -1),
                                               (below, ones, ALU.is_gt, 0.0, 1, -1),
                                               (above, ones, ALU.is_gt, 0.0, -1, 1)):
                pool.affine_select(out=dst[:, :], in_=src, compare_op=op, fill=fill, base=0,
                                   pattern=[[st, P]], channel_multiplier=cm).then_inc(const_done, 1)
            for x in range(2):
                pool.memset(hl_hi[x][:, :, H:VW].bitcast(F32), 1.0).then_inc(const_done, 1)
                pool.memset(hl_lo[x][:, :, H:VW].bitcast(F32), 0.0).then_inc(const_done, 1)
            pool.memset(hr_hi[1][:, :, H:VW].bitcast(F32), 1.0).then_inc(const_done, 1)
            pool.memset(hr_lo[1][:, :, H:VW].bitcast(F32), 0.0).then_inc(const_done, 1)

            def split_w(i, s, slot):
                n = w_index(i, s, slot)
                pool.wait_ge(w_split_hi, n + 1)
                pool.tensor_tensor(w_lo[:, slot, :, :], w_stage[:, :, :], w_hi[:, slot, :, :].bitcast(F32),
                                   ALU.subtract).then_inc(w_split_lo, 1)

            def values_lo(i, s, first, hi, lo):
                for k in range(NB):
                    n = HL_BEFORE[s] + first + k
                    pool.wait_ge(proj_hi, i * 56 + (PHI_BEFORE[s] + (6 if s < 4 else 0) + first + k + 1))
                    pool.tensor_tensor(lo[:, k, 0:H], pt[:, n % 2, 0:H], hi[:, k, 0:H].bitcast(F32),
                                       ALU.subtract).then_inc(val_lo, 1)

            def weights_lo(i, s, J):
                pool.wait_ge(weight_hi, step_count(i, s, 4, J))
                w = S if s < 4 else DW
                pool.tensor_tensor(d_lo[:, J, 0:w], td[:, J % 3, 0:w], d_hi[:, J, 0:w].bitcast(F32),
                                   ALU.subtract).then_inc(weight_lo, 1)

            def sum_exp(i, s, J):
                pool.wait_ge(exp_done, step_count(i, s, 4, J))
                if J == 1:
                    if s == 5:
                        pool.wait_ge(ring_full, job(i, 5, "z"))
                    elif late(i, 0):
                        pool.wait_ge(ring_full, job(i, 0, "z"))
                    pool.tensor_tensor(esum[:, :], td[:, 0, 0:S], td[:, 1, 0:S], ALU.add).then_inc(esum_done, 2)
                else:
                    pool.wait_ge(esum_done, i * 8 + ((s - 4) * 4 + J))
                    pool.tensor_tensor(esum[:, :], esum[:, :], td[:, J % 3, 0:S], ALU.add).then_inc(esum_done, 1)

            def weights_of(i, s, J):
                pool.wait_ge(exp_done, step_count(i, s, 4, J))
                t = td[:, J % 3, 0:S]
                pool.tensor_tensor(t, t, adjt[s % 2][:, J, :], ALU.mult).then_inc(weight_done, 1)

            def scale_shift(i, s):
                for b in range(NB):
                    if s in (3, 4):
                        pool.wait_ge(scaled, i * 8 + ((s - 3) * NB + b + 1))
                        shift = 3
                    else:
                        pool.wait_ge(normed, finished(i, s, b))
                        pool.tensor_tensor(xhat[:, b, :], xhat[:, b, :], vec[:, 7, :], ALU.mult).then_inc(pool_chain, 1)
                        chain["n"] += 1
                        pool.wait_ge(pool_chain, chain["base"] + chain["n"])
                        shift = 8
                    pool.tensor_tensor(xhat[:, b, :], xhat[:, b, :], vec[:, shift, :], ALU.add).then_inc(shifted, 1)

            def round_of_pool(i):
                for s in range(STEPS):
                    x = s % 2
                    if s < 4:
                        if x == 0:
                            split_w(i, s, 2)
                        else:
                            split_w(i, s + 1, 0)
                        values_lo(i, s, 0, hl_hi[x], hl_lo[x])
                        if x == 1:
                            split_w(i, s + 1, 1)
                        if s in (0, 3) and late(i, s):
                            scale_shift(i, s)
                        weights_of(i, s, 0)
                        weights_of(i, s, 1)
                        weights_lo(i, s, 0)
                        weights_lo(i, s, 1)
                        weights_of(i, s, 2)
                        weights_of(i, s, 3)
                        weights_lo(i, s, 2)
                        weights_lo(i, s, 3)
                    else:
                        if x == 0:
                            split_w(i, s, 2)
                        values_lo(i, s, 0, hl_hi[x], hl_lo[x])
                        if x == 1:
                            split_w(i, s + 1, 0)
                        if s == 4:
                            scale_shift(i, s)
                        values_lo(i, s, 4, hr_hi[x], hr_lo[x])
                        if s == 5:
                            scale_shift(i, s)
                        sum_exp(i, s, 1)
                        weights_lo(i, s, 0)
                        sum_exp(i, s, 2)
                        weights_lo(i, s, 1)
                        sum_exp(i, s, 3)
                        weights_lo(i, s, 2)
                        weights_lo(i, s, 3)
                        if x == 1:
                            split_w(i, s + 1, 1)

            split_w(0, 0, 0)
            split_w(0, 0, 1)
            round_of_pool(0)
            after_first = chain["n"]
            with pool.Fori(1, ROUNDS) as i:
                chain["base"], chain["n"] = i * POOL_LINKS + (after_first - POOL_LINKS), 0
                round_of_pool(i)
            assert chain["n"] == POOL_LINKS
            chain["base"], chain["n"] = after_first + (ROUNDS - 1) * POOL_LINKS, 0
            scale_shift(ROUNDS, 0)

        @block.scalar
        def _(act):
            def split_w(i, s, slot):
                n = w_index(i, s, slot)
                act.wait_ge(w_raw, n * 16 + 16)
                if not (isinstance(i, int) and i == 0 and s == 0):
                    q = s - 1
                    if q >= 0:
                        last = [("ml", 2), ("mr", 2), ("hl", 3)] if q < 4 else [("hl", 3), ("hr", 3), ("hs", 3)]
                        act.wait_ge(ring_full, job(i, q, *last[slot]))
                    else:
                        act.wait_ge(ring_full, i * JOBS_PER_ROUND)
                act.activation(w_hi[:, slot, :, :], w_stage[:, :, :], ACT.Copy).then_inc(w_split_hi, 1)

            def feature_hi(g_i, g_s, k):
                if g_s in (2, 3):
                    act.wait_ge(ht_pre, g_i * 6 + ((g_s - 2) * 3 + k + 1))
                    wait_ht_free(act, g_i, g_s, k)
                    src = pt[:, k % 2, :]
                    act.activation(ht_hi[:, k, :], src, ACT.Relu).then_inc(ht_hi_done, 1)
                    return
                if g_s in (0, 5):
                    act.wait_ge(ts_full, g_i * 6 + ((3 if g_s == 5 else 0) + k + 1))
                    src = score[k]
                else:
                    q = g_s - 1
                    act.wait_ge(ring_full, job(g_i, q, "t", k))
                    src = bank(q, "t", k)
                wait_ht_free(act, g_i, g_s, k)
                act.activation(ht_hi[:, k, :], src[:, :], ACT.Relu).then_inc(ht_hi_done, 1)

            def mixed_hi(i, s):
                for name, hi in (("ml", ml_hi), ("mr", mr_hi)):
                    for k in range(NC):
                        act.wait_ge(ring_full, job(i, s, name, k))
                        act.activation(hi[:, k, :], bank(s, name, k)[:, :], ACT.Copy).then_inc(proj_hi, 1)

            def values_hi(i, s, name, first, hi, ks=range(NB)):
                for k in ks:
                    n = HL_BEFORE[s] + first + k
                    act.wait_ge(ring_free, freed(i, s, name, k))
                    act.activation(hi[:, k, 0:H], pt[:, n % 2, 0:H], ACT.Copy).then_inc(proj_hi, 1)

            def exp_of(i, s, J):
                if s < 4:
                    act.wait_ge(masked, i * 16 + (s * 4 + J + 1))
                    act.activation(td[:, J % 3, 0:S], td[:, J % 3, 0:S], ACT.Exp).then_inc(exp_done, 1)
                else:
                    act.wait_ge(max_added, i * 8 + ((s - 4) * 4 + J + 1))
                    if J == 3:
                        act.wait_ge(weight_lo, step_count(i, s, 4, 0))
                    elif J == 0:
                        act.wait_ge(weight_lo, i * 24 + 4 * s)
                    act.activation(td[:, J % 3, 0:S], score[J][:, :], ACT.Exp, scale=ROOT_H).then_inc(exp_done, 1)

            def weight_hi_of(i, s, J):
                act.wait_ge(weight_done, step_count(i, s, 4, J))
                w = S if s < 4 else DW
                act.activation(d_hi[:, J, 0:w], td[:, J % 3, 0:w], ACT.Copy).then_inc(weight_hi, 1)

            def context_rows(i, s):
                if s == 0:
                    act.wait_ge(out_ready[0], i)
                elif s == 1 and late(i, 0):
                    act.wait_ge(out_ready[1], i)
                for b in range(NB):
                    act.wait_ge(sums_ready, contexts_read(i, s, b))
                    act.activation(xhat[:, b, :], bank(s, "c", b)[:, 0:H], ACT.Copy,
                                   scale=rden[:, b:b + 1]).then_inc(context_free, 1)

            def context_norm(i, s):
                act.wait_ge(context_scaled, i * STEPS + s)
                for b in range(NB):
                    ins = act.activation(xhat[:, b, :], xhat[:, b, :], ACT.Identity,
                                         scale=ctx_rs[:, b:b + 1], bias=ctx_nb[:, b:b + 1])
                    if s in (1, 2):
                        if b == NB - 1:
                            ins.then_inc(xhat_ready, 1)
                    else:
                        ins.then_inc(normed, 1)

            def pre_norm(n, src, dst):
                act.wait_ge(pre_scaled, n)
                for b in range(NB):
                    ins = act.activation(dst[:, b, :], src[:, b, :], ACT.Identity,
                                         scale=pre_rs[:, b:b + 1], bias=pre_nb[:, b:b + 1])
                ins.then_inc(xhat_ready, 1)

            def round_of_act(i):
                for s in range(STEPS):
                    x = s % 2
                    g_i, g_s = (i, s + 1) if s < 5 else (i + 1, 0)
                    if s < 4:
                        mixed_hi(i, s)
                        if x == 0:
                            split_w(i, s, 2)
                        else:
                            split_w(i, s + 1, 0)
                        if late(i, s):
                            context_rows(i, s)
                        values_hi(i, s, "hl", 0, hl_hi[x], range(2))
                        if late(i, s):
                            context_norm(i, s)
                        values_hi(i, s, "hl", 0, hl_hi[x], range(2, NB))
                        if s == 0:
                            pre_norm(prenorms(i, s), xnext, xnext)
                        if x == 1:
                            split_w(i, s + 1, 1)
                        exp_of(i, s, 0)
                        if s == 3:
                            pre_norm(prenorms(i, s), xres[0], xhat)
                        exp_of(i, s, 1)
                        weight_hi_of(i, s, 0)
                        weight_hi_of(i, s, 1)
                        for k in range(NC):
                            feature_hi(g_i, g_s, k)
                        exp_of(i, s, 2)
                        exp_of(i, s, 3)
                        weight_hi_of(i, s, 2)
                        weight_hi_of(i, s, 3)
                    else:
                        if x == 0:
                            split_w(i, s, 2)
                        values_hi(i, s, "hl", 0, hl_hi[x])
                        context_rows(i, s)
                        if x == 1:
                            split_w(i, s + 1, 0)
                        context_norm(i, s)
                        if s == 5:
                            pre_norm(prenorms(i, s), xnext, xnext)
                        values_hi(i, s, "hr", 4, hr_hi[x])
                        if s == 4:
                            pre_norm(prenorms(i, s), xres[1], xhat)
                        exp_of(i, s, 0)
                        exp_of(i, s, 1)
                        exp_of(i, s, 2)
                        weight_hi_of(i, s, 0)
                        exp_of(i, s, 3)
                        weight_hi_of(i, s, 1)
                        weight_hi_of(i, s, 2)
                        for k in range(NC):
                            feature_hi(g_i, g_s, k)
                        weight_hi_of(i, s, 3)
                        if x == 1:
                            split_w(i, s + 1, 1)

            pre_norm(1, xnext, xnext)
            split_w(0, 0, 0)
            for k in range(NC):
                feature_hi(0, 0, k)
            split_w(0, 0, 1)
            round_of_act(0)
            with act.Fori(1, ROUNDS) as i:
                round_of_act(i)
            context_rows(ROUNDS, 0)
            context_norm(ROUNDS, 0)

        @block.tensor
        def _(pe):
            def mm3(dst, a, b, start, stop):
                pe.matmul(dst, a[0], b[0], start=start, stop=False)
                pe.matmul(dst, a[0], b[1], start=False, stop=False)
                return pe.matmul(dst, a[1], b[0], start=False, stop=stop)

            def feat(k, lo, hi):
                return ht_hi[:, k, lo:hi], ht_lo[:, k, lo:hi]

            def weight(slot, k, lo=0, hi=H):
                return w_hi[:, slot, k, lo:hi], w_lo[:, slot, k, lo:hi]

            def wait_bank(i, s, name, k=0):
                n = JOBS[s, name, k]
                if left_out(i) and n - 4 < left_out(i):
                    pe.wait_ge(ring_free, ROUNDS * len(FREES))
                    return
                if n < 4:
                    if isinstance(i, int) and i == 0:
                        return
                    before = max(m for m in range(JOBS_PER_ROUND - 4, JOBS_PER_ROUND) if m % 4 == n)
                    pe.wait_ge(ring_free, freed(i, *JOB_AT[before]) - len(FREES))
                    return
                q, what, c = JOB_AT[n - 4]
                if what == "t":
                    pe.wait_ge(ht_lo_done, step_count(i, q + 1, 3, c))
                elif what == "c":
                    if late(i, q):
                        pe.wait_ge(context_free, contexts_read(i, q, c))
                    else:
                        pe.wait_ge(ring_free, freed(i, q, "mr", NC - 1))
                else:
                    pe.wait_ge(ring_free, freed(i, q, what, c))

            def wait_feat(i, s, k):
                pe.wait_ge(ht_hi_done, step_count(i, s, 3, k))
                pe.wait_ge(ht_lo_done, step_count(i, s, 3, k))

            def wait_weight(i, s, slot):
                pe.wait_ge(w_split_lo, w_index(i, s, slot) + 1)

            def mix_keys(i, s, name, slot, outer):
                wait_weight(i, s, slot)
                if outer:
                    for k in range(NC):
                        wait_feat(i, s, k)
                        for c in range(NC):
                            if k == 0:
                                wait_bank(i, s, name, c)
                            m = mm3(bank(s, name, c)[:, :], weight(slot, k, c * P, (c + 1) * P), feat(k, 0, S),
                                    k == 0, k == NC - 1)
                            if k == NC - 1:
                                m.then_inc(ring_full, 1)
                    return
                for c in range(NC):
                    wait_bank(i, s, name, c)
                    for k in range(NC):
                        m = mm3(bank(s, name, c)[:, :], weight(slot, k, c * P, (c + 1) * P), feat(k, 0, S),
                                k == 0, k == NC - 1)
                    m.then_inc(ring_full, 1 if late(i, s) or c < NC - 1 else 1 + 1 + NB)

            def values(i, s, name, slot):
                wait_weight(i, s, slot)
                for b in range(NB):
                    wait_bank(i, s, name, b)
                    for k in range(NC):
                        m = mm3(bank(s, name, b)[:, 0:H], feat(k, b * P, (b + 1) * P), weight(slot, k),
                                k == 0, k == NC - 1)
                    m.then_inc(ring_full, 1)

            def values_outer(i, s, name, slot, ks, free_feat):
                for k in ks:
                    if k == 0:
                        wait_weight(i, s, slot)
                    if not free_feat:
                        wait_feat(i, s, k)
                    for b in range(NB):
                        if k == 0:
                            wait_bank(i, s, name, b)
                        m = mm3(bank(s, name, b)[:, 0:H], feat(k, b * P, (b + 1) * P), weight(slot, k),
                                k == 0, k == NC - 1)
                        if k == NC - 1:
                            m.then_inc(ring_full, 1)
                    if free_feat and k < NC - 1:
                        m.then_inc(ht_free, 1)

            def exp_sums(i, s):
                wait_bank(i, s, "z")
                pe.wait_ge(esum_done, (i * 8 + 4) if s == 5 else i * 8)
                for b in range(NB):
                    m = pe.matmul(bank(s, "z")[:, b:b + 1], esum[:, b * P:(b + 1) * P], ones[:, 0:1],
                                  start=True, stop=True)
                m.then_inc(ring_full, 1)

            def context(i, s):
                q = (s - 1) % STEPS
                x = q % 2
                qi = i if s else i - 1
                values_before = (qi * 32) + HL_BEFORE[q] + (4 if q < 4 else 8)
                pe.wait_ge(val_lo, values_before)
                for b in range(NB):
                    wait_bank(i, s, "c", b)
                    terms = []
                    for J in range(NB):
                        cols = slice(b * P, (b + 1) * P)
                        if q < 4 or J > b:
                            terms.append((J, cols, hl_hi[x], hl_lo[x]))
                        elif J == b:
                            terms.append((J, cols, hl_hi[x], hl_lo[x]))
                            terms.append((J, slice(S, DW), hr_hi[x], hr_lo[x]))
                        else:
                            terms.append((J, cols, hr_hi[x], hr_lo[x]))
                    for n, (J, cols, vh, vl) in enumerate(terms):
                        if b == 0:
                            pe.wait_ge(weight_lo, step_count(qi, q, 4, J))
                        m = mm3(bank(s, "c", b)[:, 0:VW], (d_hi[:, J, cols], d_lo[:, J, cols]),
                                (vh[:, J, :], vl[:, J, :]), n == 0, n == len(terms) - 1)
                    m.then_inc(ring_full, 1)

            def transposes(i, s, k, dst, full):
                src = xnext if s in (5, 0, -1) else xhat
                if k == 0:
                    pe.wait_ge(xhat_ready, step_count(i, s, 1) + 1)
                for b in range(NB):
                    m = pe.transpose(dst[:, b * P:(b + 1) * P], src[:, b, k * P:(k + 1) * P], ident[:, :])
                m.then_inc(full, 1)

            def edge_scores(i, s, J, ks, free):
                left, right = score[2 * (J % 2)], score[2 * (J % 2) + 1]
                lw = max(MIN_N, (J + 1) * P)
                rl = min(S - MIN_N, J * P)
                for k in ks:
                    mm3(left[:, 0:lw], (ml_hi[:, k, J * P:(J + 1) * P], ml_lo[:, k, J * P:(J + 1) * P]),
                        feat(k, 0, lw), k == 0, k == NC - 1)
                    m = mm3(right[:, rl:S], (mr_hi[:, k, J * P:(J + 1) * P], mr_lo[:, k, J * P:(J + 1) * P]),
                            feat(k, rl, S), k == 0, k == NC - 1)
                    if k == NC - 1:
                        m.then_inc(score_full, 1)
                    elif free:
                        m.then_inc(ht_free, 1)

            def edge_step(i, s):
                mix_keys(i, s, "ml", 0, True)
                mix_keys(i, s, "mr", 1, False)
                if late(i, s):
                    if s == 0:
                        exp_sums(i, s)
                    context(i, s)
                values(i, s, "hl", 2)
                pe.wait_ge(ring_free, freed(i, s, "mr", 2))
                if s > 0:
                    pe.wait_ge(masked, i * 16 + 4 * s)
                else:
                    if late(i, s):
                        pe.wait_ge(exp_done, i * 24)
                    pe.wait_ge(ht_lo_done, i * 18 + 3)
                edge_scores(i, s, 0, range(NC), False)
                edge_scores(i, s, 1, range(NC), False)
                for k in range(NC):
                    if k == 0:
                        pe.wait_ge(masked, i * 16 + (4 * s + 1))
                    edge_scores(i, s, 2, [k], False)
                    if k == 0:
                        pe.wait_ge(masked, i * 16 + (4 * s + 2))
                    edge_scores(i, s, 3, [k], True)
                    if k == 0:
                        for c in range(NC):
                            if s == 3 or True:
                                wait_bank(i, s, "t", c)
                            transposes(i, s, c, bank(s, "t", c), ring_full)

            def soft_step(i, s):
                values_outer(i, s, "hl", 0, range(NC), False)
                if s == 5:
                    exp_sums(i, s)
                context(i, s)
                if s == 4:
                    pe.wait_ge(masked, i * 16 + 16)
                else:
                    pe.wait_ge(exp_done, i * 24 + 20)
                    pe.wait_ge(ht_lo_done, i * 18 + 18 - 0)
                for J in range(NB):
                    for k in range(NC):
                        m = mm3(score[J][:, :], feat(k, J * P, (J + 1) * P), feat(k, 0, S), k == 0, k == NC - 1)
                    m.then_inc(score_full, 1)
                values(i, s, "hr", 1)
                pe.wait_ge(max_ready, i * 2 + (s - 3))
                for J in range(NB):
                    pe.matmul(score[J][:, :], ones_r[:, :], negmax[:, :, :].rearrange("p b q -> p (b q)"),
                              start=False, stop=True, skip_group_check=True).then_inc(max_added, 1)
                values_outer(i, s, "hs", 2, range(NC - 1), True)
                for c in range(NC):
                    pe.wait_ge(exp_done, step_count(i, s, 4, c))
                    transposes(i, s, c, score[c], ts_full)
                values_outer(i, s, "hs", 2, [NC - 1], True)

            def round_of_pe(i):
                for s in range(4):
                    edge_step(i, s)
                for s in range(4, STEPS):
                    soft_step(i, s)

            pe.wait_ge(const_done, 10)
            for c in range(NC):
                transposes(0, -1, c, score[c], ts_full)
            round_of_pe(0)
            with pe.Fori(1, ROUNDS) as i:
                round_of_pe(i)
            exp_sums(ROUNDS, 0)
            context(ROUNDS, 0)

        @block.vector
        def _(dve):
            chain = {"base": 0, "n": 0}

            def link(ins):
                ins.then_inc(dve_chain, 1)
                chain["n"] += 1
                dve.wait_ge(dve_chain, chain["base"] + chain["n"])

            def rsqrt(dst):
                link(dve.tensor_scalar(nt.bitcast(I32), var.bitcast(I32), 1, None, ALU.logical_shift_right))
                link(dve.tensor_scalar(dst.bitcast(I32), nt.bitcast(I32), -1.0, NEG_HALF_MAGIC, ALU.mult, ALU.add))
                for _ in range(4):
                    link(dve.tensor_tensor(nt, dst, dst, ALU.mult))
                    link(dve.scalar_tensor_tensor(nt, nt, -0.5, var, ALU.mult, ALU.mult))
                    link(dve.scalar_tensor_tensor(dst, nt, 1.5, dst, ALU.add, ALU.mult))

            def row_moments():
                mean_e, mean_o, ssd_e, ssd_o = (stats[:, :, q] for q in (1, 4, 2, 5))
                dve.tensor_tensor(msum, mean_e, mean_o, ALU.add).then_inc(dve_chain, 1)
                dve.tensor_tensor(nt, mean_e, mean_o, ALU.subtract).then_inc(dve_chain, 1)
                chain["n"] += 2
                link(dve.tensor_tensor(var, ssd_e, ssd_o, ALU.add))
                link(dve.scalar_tensor_tensor(nt, nt, 0.25, nt, ALU.mult, ALU.mult))
                link(dve.scalar_tensor_tensor(var, var, 1.0 / H, nt, ALU.mult, ALU.add))

            def pre_scale():
                row_moments()
                link(dve.tensor_scalar(var, var, 1e-5, None, ALU.add))
                rsqrt(pre_rs)
                dve.scalar_tensor_tensor(pre_nb, msum, -0.5, pre_rs, ALU.mult, ALU.mult).then_inc(pre_scaled, 1)

            def load_norm(n, n_before):
                dve.wait_ge(xnext_in, n)
                for b in range(NB):
                    ins = dve.bn_stats(stats[:, b, :], xnext[:, b, :])
                link(ins)
                if n_before is not None:
                    dve.wait_ge(xhat_ready, n_before)
                pre_scale()

            def edge_rows(i, s):
                if not (isinstance(i, int) and i == 0 and s == 1):
                    dve.wait_ge(context_free, contexts_read(i, s - 1, NB - 1))
                for b in range(NB):
                    src = bank(s, "c", b)
                    dve.wait_ge(ring_full, job(i, s, "c", b))
                    link(dve.tensor_scalar(den[:, b:b + 1], src[:, H:H + 1], 1e-10, None, ALU.add))
                    dve.reciprocal(rden[:, b:b + 1], den[:, b:b + 1]).then_inc(sums_ready, 1)
                    if b > 0:
                        dve.wait_ge(context_free, contexts_read(i, s, b - 1))
                        dve.bn_stats(stats[:, b - 1, :], xhat[:, b - 1, :])
                dve.wait_ge(context_free, contexts_read(i, s, NB - 1))
                link(dve.bn_stats(stats[:, NB - 1, :], xhat[:, NB - 1, :]))

            def edge_scale(i, s):
                row_moments()
                link(dve.tensor_scalar(var, var, H / (H - 1.0), 1e-30, ALU.mult, ALU.max))
                rsqrt(den)
                link(dve.tensor_tensor(nt, var, den, ALU.mult))
                link(dve.tensor_scalar(nt, nt, 1e-3, None, ALU.add))
                if s == 1:
                    if late(i, 0):
                        dve.wait_ge(normed, finished(i, 0, NB - 1))
                elif s in (2, 3):
                    dve.wait_ge(xhat_ready, i * STEPS + (s + 1))
                else:
                    dve.wait_ge(normed, finished(i, s - 1, NB - 1))
                link(dve.reciprocal(ctx_rs, nt))
                dve.scalar_tensor_tensor(ctx_nb, msum, -0.5, ctx_rs, ALU.mult, ALU.mult).then_inc(context_scaled, 1)

            def scale(i, s):
                for b in range(NB):
                    dve.wait_ge(normed, finished(i, s, b))
                    dve.tensor_tensor(xhat[:, b, :], xhat[:, b, :], vec[:, 2, :], ALU.mult).then_inc(scaled, 1)

            def residual(i, s):
                x = (s - 1) % 2
                if s == 3 or s == 4:
                    dve.wait_ge(xres_in[x], i * 16 + 16)
                for b in range(NB):
                    dve.wait_ge(shifted, finished(i, s, b))
                    ins = dve.scalar_tensor_tensor(xres[x][:, b, :], xhat[:, b, :], 0.0, xres[x][:, b, :],
                                                   ALU.max, ALU.add)
                    if s in (3, 4):
                        link(ins)
                        ins = dve.bn_stats(stats[:, b, :], xres[x][:, b, :])
                        if b == NB - 1:
                            link(ins)
                    elif b == NB - 1:
                        ins.then_inc(out_ready[x], 1)

            def soft_rows(i, s):
                x = (s - 1) % 2
                dd = diag[:, x, :]
                dve.wait_ge(ring_full, job(i, s, "z"))
                dve.tensor_copy(zc, bank(s, "z")[:, 0:NB]).then_inc(ring_free, 1)
                dve.wait_ge(ring_free, freed(i, s, "z"))
                dve.wait_ge(context_free, contexts_read(i, s, 0) - 1)
                for b in range(NB):
                    src = bank(s, "c", b)
                    c = slice(b, b + 1)
                    dve.wait_ge(ring_full, job(i, s, "c", b))
                    link(dve.scalar_tensor_tensor(den[:, c], zc[:, c], 1e-10, src[:, H:H + 1], ALU.mult, ALU.add))
                    link(dve.tensor_tensor(den[:, c], den[:, c], dd[:, c], ALU.add))
                    dve.reciprocal(rden[:, c], den[:, c]).then_inc(sums_ready, 1)
                    dve.wait_ge(sums_ready, contexts_read(i, s, b))
                    link(dve.tensor_tensor(ddr[:, c], dd[:, c], rden[:, c], ALU.mult))
                    dve.wait_ge(context_free, contexts_read(i, s, b))
                    link(dve.scalar_tensor_tensor(xhat[:, b, :], hs[x][:, b, :], ddr[:, c], xhat[:, b, :],
                                                  ALU.mult, ALU.add))
                    ins = dve.bn_stats(stats[:, b, :], xhat[:, b, :])
                link(ins)

            def soft_scale(i, s):
                row_moments()
                link(dve.tensor_scalar(var, var, 1e-12, None, ALU.add))
                dve.wait_ge(normed, finished(i, s, 0) - 1)
                rsqrt(ctx_rs)
                dve.scalar_tensor_tensor(ctx_nb, msum, -0.5, ctx_rs, ALU.mult, ALU.mult).then_inc(context_scaled, 1)

            def feature_lo(g_i, g_s, k):
                in_ring = g_s not in (0, 5)
                src = bank(g_s - 1, "t", k) if in_ring else score[k]
                if g_s in (2, 3):
                    dve.wait_ge(ring_full, job(g_i, g_s - 1, "t", k))
                    if k < 2:
                        dve.wait_ge(val_lo, g_i * 32 + (HL_BEFORE[g_s]))
                    else:
                        dve.wait_ge(ht_lo_done, step_count(g_i, g_s, 3, 0))
                    dve.tensor_scalar(pt[:, k % 2, :], src[:, :], lnab[:, 0, k:k + 1], lnab[:, 1, k:k + 1],
                                      ALU.mult, ALU.add).then_inc(ht_pre, 1)
                    dve.wait_ge(ht_hi_done, step_count(g_i, g_s, 3, k))
                    ins = dve.scalar_tensor_tensor(ht_lo[:, k, :], pt[:, k % 2, :], 0.0,
                                                   ht_hi[:, k, :].bitcast(F32), ALU.max, ALU.subtract)
                else:
                    dve.wait_ge(ht_hi_done, step_count(g_i, g_s, 3, k))
                    ins = dve.scalar_tensor_tensor(ht_lo[:, k, :], src[:, :], 0.0,
                                                   ht_hi[:, k, :].bitcast(F32), ALU.max, ALU.subtract)
                ins.then_inc(ht_lo_done, 1)

            def mixed_lo(i, s):
                for first, name, hi, lo in ((0, "ml", ml_hi, ml_lo), (NC, "mr", mr_hi, mr_lo)):
                    for k in range(NC):
                        dve.wait_ge(proj_hi, i * 56 + (PHI_BEFORE[s] + first + k + 1))
                        skipped = 0 if late(i, s) or name == "ml" or k < NC - 1 else 1
                        dve.tensor_tensor(lo[:, k, :], bank(s, name, k)[:, :], hi[:, k, :].bitcast(F32),
                                          ALU.subtract).then_inc(ring_free, 1 + skipped)

            def values_bias(i, s, name, first, bias, ks=range(NB)):
                for k in ks:
                    n = HL_BEFORE[s] + first + k
                    dve.wait_ge(ring_full, job(i, s, name, k))
                    if not (isinstance(i, int) and i == 0 and n < 2):
                        dve.wait_ge(val_lo, i * 32 + (n - 1))
                    dve.tensor_tensor(pt[:, n % 2, 0:H], bank(s, name, k)[:, 0:H], vec[:, bias, :],
                                      ALU.add).then_inc(ring_free, 1)

            def mask_of(i, s, J):
                x = s % 2
                left, right = score[2 * (J % 2)], score[2 * (J % 2) + 1]
                lo, hi = J * P, (J + 1) * P
                t = td[:, J % 3, :]
                dve.wait_ge(score_full, step_count(i, s, 4, J))
                if J == 0 and not (isinstance(i, int) and i == 0 and s == 0):
                    dve.wait_ge(weight_lo, i * 24 + 4 * s)
                elif J == 3:
                    dve.wait_ge(weight_lo, step_count(i, s, 4, 0))
                if J > 0:
                    dve.scalar_tensor_tensor(t[:, 0:lo], left[:, 0:lo], ROOT_H, adjt[x][:, J, 0:lo], ALU.mult, ALU.mult)
                    rest = slice(lo, S)
                else:
                    dve.scalar_tensor_tensor(t[:, P:S], right[:, P:S], ROOT_H, adjn[x][:, P:S], ALU.mult, ALU.mult)
                    rest = slice(0, P)
                link(dve.copy_predicated(right[:, lo:hi], low[:, :].bitcast(I32), left[:, lo:hi]))
                dve.scalar_tensor_tensor(t[:, rest], right[:, rest], ROOT_H,
                                         adjn[x][:, AT[J]:AT[J] + rest.stop - rest.start],
                                         ALU.mult, ALU.mult).then_inc(masked, 1)

            def weight_of(i, s, J):
                x = s % 2
                t = td[:, J % 3, :]
                dve.wait_ge(exp_done, step_count(i, s, 4, J))
                lo, hi = J * P, (J + 1) * P
                dve.wait_ge(esum_done, i * 8 + ((s - 4) * 4 + J + 1))
                link(dve.tensor_tensor(t[:, 0:S], t[:, 0:S], adjt[x][:, J, :], ALU.mult))
                link(dve.scalar_tensor_tensor(t[:, S:DW], t[:, lo:hi], 1.0, ident[:, :], ALU.mult, ALU.mult,
                                              accum_out=diag[:, x, J:J + 1]))
                link(dve.tensor_tensor(t[:, S:DW], t[:, lo:hi], above[:, :], ALU.mult))
                dve.tensor_tensor(t[:, lo:hi], t[:, lo:hi], below[:, :], ALU.mult).then_inc(weight_done, 1)

            def maxima(i, s):
                for J in range(NB):
                    dve.wait_ge(score_full, step_count(i, s, 4, J))
                    link(dve.tensor_reduce(mx[:, J:J + 1], score[J][:, :], AX_X, ALU.max))
                if s == 5:
                    dve.wait_ge(max_added, i * 8 + 4)
                elif late(i, 0):
                    dve.wait_ge(max_added, i * 8)
                for J in range(NB):
                    ins = dve.tensor_scalar(negmax[:, J, :], ident[:, :], mx[:, J:J + 1], -1.0, ALU.mult, ALU.mult)
                    if J == NB - 1:
                        ins.then_inc(max_ready, 1)
                    else:
                        link(ins)

            def mirror_adj(i, x):
                for J in range(NB):
                    ins = dve.copy_predicated(adjn[x][:, AT[J]:AT[J] + P], low[:, :].bitcast(I32),
                                              adjt[x][:, J, J * P:(J + 1) * P])
                link(ins)

            def round_of_dve(i):
                for s in range(STEPS):
                    x = s % 2
                    g_i, g_s = (i, s + 1) if s < 5 else (i + 1, 0)
                    if s < 4:
                        if s < 2:
                            dve.wait_ge(adj_in_sem[x], i * 80 + 80)
                        mixed_lo(i, s)
                        if s > 0:
                            edge_rows(i, s)
                            edge_scale(i, s)
                        elif late(i, s):
                            soft_rows(i, s)
                            soft_scale(i, s)
                        values_bias(i, s, "hl", 0, s // 2, range(2))
                        if s == 3:
                            scale(i, s)
                        values_bias(i, s, "hl", 0, s // 2, range(2, NB))
                        if s < 2:
                            mirror_adj(i, x)
                        if s == 0:
                            load_norm(i * 32 + 32, i * STEPS + 1)
                        if s == 3:
                            residual(i, s)
                            dve.wait_ge(xhat_ready, i * STEPS + 2)
                            pre_scale()
                        mask_of(i, s, 0)
                        mask_of(i, s, 1)
                        if s == 0 and late(i, s):
                            residual(i, s)
                        for k in range(NC):
                            feature_lo(g_i, g_s, k)
                        mask_of(i, s, 2)
                        mask_of(i, s, 3)
                    else:
                        values_bias(i, s, "hl", 0, 4)
                        if s == 4:
                            edge_rows(i, s)
                            edge_scale(i, s)
                            scale(i, s)
                        else:
                            soft_rows(i, s)
                            soft_scale(i, s)
                            load_norm(i * 32 + 48, i * STEPS + 6)
                        maxima(i, s)
                        if s == 4:
                            residual(i, s)
                            dve.wait_ge(xhat_ready, i * STEPS + 5)
                            pre_scale()
                        dve.wait_ge(ring_full, job(i, s, "hr", 0))
                        if s == 4:
                            link(dve.memset(hr_hi[0][:, :, H:VW].bitcast(F32), 1.0))
                            link(dve.memset(hr_lo[0][:, :, H:VW].bitcast(F32), 0.0))
                        values_bias(i, s, "hr", 4, 5)
                        for J in range(NB):
                            weight_of(i, s, J)
                        for k in range(NC):
                            feature_lo(g_i, g_s, k)
                        if s == 5:
                            residual(i, s)
                        for b in range(NB):
                            dve.wait_ge(ring_full, job(i, s, "hs", b))
                            dve.tensor_tensor(hs[x][:, b, :], bank(s, "hs", b)[:, 0:H], vec[:, 6, :],
                                              ALU.add).then_inc(ring_free, 1)

            dve.wait_ge(const_done, 10)
            load_norm(16, None)
            for k in range(NC):
                feature_lo(0, 0, k)
            dve.wait_ge(vec_in_sem, 32)
            round_of_dve(0)
            after_first = chain["n"]
            chain["n"] = 0
            per_round = DVE_LINKS
            with dve.Fori(1, ROUNDS) as i:
                chain["base"] = i * per_round + (after_first - per_round)
                round_of_dve(i)
            assert chain["n"] == per_round, chain["n"]
            chain["base"] = after_first + (ROUNDS - 1) * per_round
            chain["n"] = 0
            soft_rows(ROUNDS, 0)
            soft_scale(ROUNDS, 0)
            residual(ROUNDS, 0)


DVE_LINKS = 336
POOL_LINKS = 8


def kernel(x, adj, L0_gnn_W_left, L0_gnn_W_right, L0_gnn_W_lin, L0_gnn_b_lin, L0_gnn_ln_a, L0_gnn_ln_b,
           L1_gnn_W_left, L1_gnn_b_left, L1_gnn_W_self, L1_gnn_b_self, L1_gnn_W_right, L1_gnn_b_right,
           L1_gnn_gamma, L1_gnn_beta):
    import numpy as np
    import concourse.bacc as bacc
    from concourse.bass_utils import run_bass_kernel_spmd

    f = np.ascontiguousarray
    w = f(np.stack([np.swapaxes(np.asarray(m), 0, 1) for m in (
        L0_gnn_W_left[0], L0_gnn_W_right[0], L0_gnn_W_lin[0],
        L0_gnn_W_left[1], L0_gnn_W_right[1], L0_gnn_W_lin[1],
        L1_gnn_W_left, L1_gnn_W_right, L1_gnn_W_self)]).reshape(3, 3, H, H))
    vec = np.stack([np.asarray(v) for v in (
        L0_gnn_b_lin[0], L0_gnn_b_lin[1], L0_gnn_ln_a[1], L0_gnn_ln_b[1],
        L1_gnn_b_left, L1_gnn_b_right, L1_gnn_b_self, L1_gnn_gamma, L1_gnn_beta)])
    vec = f(np.broadcast_to(vec[None], (P, 9, H)))
    lnab = f(np.stack([np.asarray(L0_gnn_ln_a[0]).reshape(NC, P),
                       np.asarray(L0_gnn_ln_b[0]).reshape(NC, P)]).transpose(2, 0, 1))
    arrays = {"x": f(x), "adj": f(adj), "adjt": f(np.swapaxes(np.asarray(adj), 1, 2)), "w": w, "vec": vec,
              "lnab": lnab}
    nc = bacc.Bacc("TRN2", target_bir_lowering=False, num_devices=1)
    args = [nc.dram_tensor(f"in_{n}", a.shape, mybir.dt.from_np(a.dtype), kind="ExternalInput").ap()
            for n, a in arrays.items()]
    out = nc.dram_tensor("out", (B, S, H), F32, kind="ExternalOutput").ap()
    gnn_kernel(nc, *args, out)
    r = run_bass_kernel_spmd(nc, [{f"in_{n}": a for n, a in arrays.items()}], core_ids=[0])
    return r.results[0]["out"]
```

```python
from contextlib import ExitStack

import concourse.bass as bass
from concourse import mybir

F32 = mybir.dt.float32
F32R = mybir.dt.float32r
I32 = mybir.dt.int32
ALU = mybir.AluOpType
ACT = mybir.ActivationFunctionType
AX_X = mybir.AxisListType.X

P = 128
B, S, H = 16, 512, 384
NB = S // P
NC = H // P
VW = H + 2
DW = S + P
STEPS = 6
ROUNDS = B // 2
ROOT_H = float(H) ** -0.5
MIN_N = 256
RSQRT_GUESS = float(0x5F3759DF)


def job_table():
    table, frees, n = {}, {}, 0
    for s in range(STEPS):
        if s == 3:
            order = [("ml", NC), ("c", NB), ("mr", NC), ("hl", NB), ("t", NC)]
        elif s < 4:
            order = [("ml", NC), ("mr", NC)] + ([("z", 1)] if s == 0 else []) + [("c", NB), ("hl", NB), ("t", NC)]
        else:
            order = [("hl", NB), ("c", NB), ("hr", NB), ("hs", NB)]
        for name, count in order:
            for k in range(count):
                if (s, name, k) == (5, "c", 1):
                    table[s, "z", 0], frees[s, "z", 0] = n, len(frees)
                    n += 1
                table[s, name, k] = n
                n += 1
                if name not in ("t", "c"):
                    frees[s, name, k] = len(frees)
    return table, n, frees


JOBS, JOBS_PER_ROUND, FREES = job_table()
JOB_AT = {n: key for key, n in JOBS.items()}
HL_BEFORE = [4 * s if s < 4 else 16 + 8 * (s - 4) for s in range(STEPS)]
PHI_BEFORE = [10 * s if s < 4 else 40 + 8 * (s - 4) for s in range(STEPS)]


def gnn_kernel(nc, x_in, adj_in, adjt_in, w_in, vec_in, lnab_in, out):
    with ExitStack() as ctx:
        def sb(name, shape, dt=F32):
            return ctx.enter_context(nc.sbuf_tensor(name, shape, dt))

        def sem(name):
            return ctx.enter_context(nc.semaphore(name))

        ring = [ctx.enter_context(nc.psum_tensor(f"ring{k}", [P, 512], F32)) for k in range(4)]
        score = [ctx.enter_context(nc.psum_tensor(f"score{k}", [P, 512], F32)) for k in range(4)]

        w_stage = sb("w_stage", [P, NC, H])
        w_hi = sb("w_hi", [P, 3, NC, H], F32R)
        w_lo = sb("w_lo", [P, 3, NC, H], F32R)
        vec = sb("vec", [P, 9, H])
        lnab = sb("lnab", [P, 2, NC])
        ht_hi = sb("ht_hi", [P, NC, S], F32R)
        ht_lo = sb("ht_lo", [P, NC, S], F32R)
        mix = sb("mix", [P, 4 * NC * S], F32R)
        ml_hi, ml_lo, mr_hi, mr_lo = (
            mix[:, q * NC * S:(q + 1) * NC * S].rearrange("p (c s) -> p c s", c=NC) for q in range(4))
        hl_hi = [sb(f"hl_hi{x}", [P, NB, VW], F32R) for x in range(2)]
        hl_lo = [sb(f"hl_lo{x}", [P, NB, VW], F32R) for x in range(2)]
        hrb = sb("hrb", [P, 2 * NB * VW], F32R)
        hr_hi, hr_lo = ([r[:, q * NB * VW:(q + 1) * NB * VW].rearrange("p (b v) -> p b v", b=NB)
                         for r in (mix, hrb)] for q in range(2))
        d_hi = sb("d_hi", [P, NB, DW], F32R)
        d_lo = sb("d_lo", [P, NB, DW], F32R)
        adjt = [sb(f"adjt{x}", [P, NB, S]) for x in range(2)]
        adjn = [sb(f"adjn{x}", [P, NB * H]) for x in range(2)]
        hs = [adjn[x][:, :].rearrange("p (b v) -> p b v", b=NB) for x in range(2)]
        AT = [sum(S - P * k for k in range(J)) for J in range(NB + 1)]
        xres = [sb(f"xres{x}", [P, NB, H]) for x in range(2)]
        xnext = sb("xnext", [P, NB, H])
        xhat = sb("xhat", [P, NB, H])
        td = sb("td", [P, 3, DW])
        esum = sb("esum", [P, S])
        pt = sb("pt", [P, 2, S])
        maxdiag = sb("maxdiag", [P, NB, P], F32R)
        ident = sb("ident", [P, P])
        low = sb("low", [P, P])
        below = sb("below", [P, P])
        above = sb("above", [P, P])
        minus_r = sb("minus_r", [P, P], F32R)
        stats = sb("stats", [P, NB, 6])
        stats_in = sb("stats_in", [P, NB, 6])
        small = sb("small", [P, 16, NB])
        den, rden, var, nt, mx, zc, ddr, msum = (small[:, k, :] for k in range(8))
        ctx_rs, ctx_nb, pre_rs, pre_nb = (small[:, k, :] for k in range(8, 12))
        diag = small[:, 12:14, :]

        const_done = sem("const_done")
        vec_in_sem = sem("vec_in_sem")
        w_raw = sem("w_raw")
        xnext_in = sem("xnext_in")
        xres_in = [sem(f"xres_in{x}") for x in range(2)]
        adj_in_sem = [sem(f"adj_in{x}") for x in range(2)]
        w_split_hi = sem("w_split_hi")
        w_split_lo = sem("w_split_lo")
        ring_full = sem("ring_full")
        ring_free = sem("ring_free")
        sums_ready = sem("sums_ready")
        context_free = sem("context_free")
        context_scaled = sem("context_scaled")
        normed = sem("normed")
        scaled = sem("scaled")
        shifted = sem("shifted")
        pre_scaled = sem("pre_scaled")
        xhat_ready = sem("xhat_ready")
        xnext_ready = sem("xnext_ready")
        ht_pre = sem("ht_pre")
        ht_hi_done = sem("ht_hi_done")
        ht_lo_done = sem("ht_lo_done")
        ht_free = sem("ht_free")
        ts_full = sem("ts_full")
        proj_hi = sem("proj_hi")
        val_lo = sem("val_lo")
        score_full = sem("score_full")
        masked = sem("masked")
        exp_done = sem("exp_done")
        esum_done = sem("esum_done")
        weight_done = sem("weight_done")
        weight_hi = sem("weight_hi")
        weight_lo = sem("weight_lo")
        max_ready = sem("max_ready")
        diag_ready = sem("diag_ready")
        max_added = sem("max_added")
        adjn_ready = sem("adjn_ready")
        hs_ready = sem("hs_ready")
        out_ready = [sem(f"out_ready{x}") for x in range(2)]
        out_done = [sem(f"out_done{x}") for x in range(2)]
        dve_chain = sem("dve_chain")
        pool_chain = sem("pool_chain")

        def left_out(i):
            return 2 * NC if isinstance(i, int) and i == ROUNDS else 0

        def job(i, s, name, k=0):
            return i * JOBS_PER_ROUND + (JOBS[s, name, k] + 1 - left_out(i))

        def freed(i, s, name, k=0):
            return i * len(FREES) + (FREES[s, name, k] + 1 - left_out(i))

        def contexts_read(i, s, b):
            return i * (STEPS * NB) + (s * NB + b + 1 - NB)

        def finished(i, s, b):
            return i * (4 * NB) + ({0: 0, 3: NB, 4: 2 * NB, 5: 3 * NB}[s] + b + 1 - NB)

        def prenorms(i, s):
            return i * 4 + ({0: 0, 2: 1, 3: 2, 4: 3}[s] + 2)

        def rows_ready(i, s, b):
            return i * (4 * NB) + ((s - 1) * NB + b + 1)

        def next_ready(i, s, b):
            return i * (2 * NB) + ((NB if s == 0 else 2 * NB) + b + 1)

        def bank(s, name, k=0):
            return ring[JOBS[s, name, k] % 4]

        def step_count(i, s, per, k=0):
            return i * (STEPS * per) + (s * per + k + 1)

        def late(i, s):
            return not (isinstance(i, int) and i == 0 and s == 0)

        def wait_ht_free(eng, g_i, g_s, k):
            if isinstance(g_i, int) and g_i == 0 and g_s == 0:
                return
            if k < NC - 1:
                eng.wait_ge(ht_free, g_i * (2 * STEPS) + (2 * g_s - 2 + k + 1))
            elif g_s == 0:
                eng.wait_ge(ring_full, g_i * JOBS_PER_ROUND)
            elif g_s == 5:
                eng.wait_ge(ring_full, job(g_i, 4, "hs", NB - 1))
            else:
                eng.wait_ge(score_full, step_count(g_i, g_s - 1, 4, 3))

        def w_index(i, s, slot):
            return i * 9 + (3 * (s // 2) + slot)

        def xrows(i, x):
            return x_in[bass.ds(i, 1), :, :].rearrange("a (b p) h -> p (a b) h", p=P)

        block = ctx.enter_context(nc.Block())

        @block.sync
        def _(sp):
            def load_w(i, s, slot):
                n = w_index(i, s, slot)
                if not (isinstance(n, int) and n == 0):
                    sp.wait_ge(w_split_lo, n)
                layer = (s // 2) % 3
                sp.dma_start(w_stage[:, :, :], w_in[layer, slot].rearrange("(c p) o -> p c o", p=P)).then_inc(w_raw, 16)

            def load_adj(b, x):
                sp.dma_start(adjt[x][:, :, :],
                             adjt_in[bass.ds(b, 1), :, :].rearrange("a (b p) s -> p (a b) s", p=P)).then_inc(adj_in_sem[x], 16)
                for J in range(NB):
                    sp.dma_start(adjn[x][:, AT[J]:AT[J + 1]],
                                 adj_in[bass.ds(b, 1), J * P:(J + 1) * P, J * P:S].rearrange("a p s -> (a p) s")
                                 ).then_inc(adj_in_sem[x], 16)

            def load_xnext(b):
                sp.dma_start(xnext[:, :, :], xrows(b, 0)).then_inc(xnext_in, 16)

            def load_xres(b, x):
                sp.dma_start(xres[x][:, :, :], xrows(b, x)).then_inc(xres_in[x], 16)

            def store(b, x):
                sp.dma_start(out[bass.ds(b, 1), :, :].rearrange("a (b p) h -> p (a b) h", p=P),
                             xres[x][:, :, :]).then_inc(out_done[x], 16)

            def round_of_loads(i, last):
                load_w(i, 0, 2)
                if not late(i, 0):
                    sp.dma_start(vec[:, :, :], vec_in).then_inc(vec_in_sem, 16)
                    load_adj(0, 0)
                    sp.dma_start(lnab[:, :, :], lnab_in).then_inc(vec_in_sem, 16)
                    load_adj(1, 1)
                    load_xres(0, 0)
                    load_xres(1, 1)
                else:
                    sp.wait_ge(out_ready[0], i)
                    store(i * 2 - 2, 0)
                    sp.wait_ge(context_scaled, i * STEPS)
                    load_adj(i * 2 + 1, 1)
                load_w(i, 2, 0)
                if late(i, 0):
                    sp.wait_ge(out_done[0], i * 16)
                    load_xres(i * 2, 0)
                sp.wait_ge(ring_full, job(i, 0, "t", 2))
                load_xnext(0 if last else i * 2 + 2)
                load_w(i, 2, 1)
                if late(i, 0):
                    sp.wait_ge(out_ready[1], i)
                    store(i * 2 - 1, 1)
                load_w(i, 2, 2)
                if late(i, 0):
                    sp.wait_ge(out_done[1], i * 16)
                    load_xres(i * 2 + 1, 1)
                load_w(i, 4, 0)
                load_w(i, 4, 1)
                load_w(i, 4, 2)
                load_w(i, 6, 0)
                if not last:
                    sp.wait_ge(context_scaled, i * STEPS + 5)
                    load_adj(i * 2 + 2, 0)
                load_w(i, 6, 1)
                if not last:
                    sp.wait_ge(ts_full, i * 6 + 9)
                    load_xnext(i * 2 + 3)

            sp.dma_start(xnext[:, :, :], xrows(0, 0)).then_inc(xnext_in, 16)
            load_w(0, 0, 0)
            load_w(0, 0, 1)
            sp.wait_ge(ts_full, 3)
            load_xnext(1)
            round_of_loads(0, False)
            with sp.Fori(1, ROUNDS - 1) as i:
                round_of_loads(i, False)
            round_of_loads(ROUNDS - 1, True)
            sp.wait_ge(out_ready[0], ROUNDS)
            store(B - 2, 0)
            for b in range(NB):
                sp.wait_ge(out_ready[1], ROUNDS + b)
                sp.dma_start(out[B - 1, b * P:(b + 1) * P, :], xres[1][:, b, :]).then_inc(out_done[1], 16)
            sp.wait_ge(out_done[0], 16 * ROUNDS)
            sp.wait_ge(out_done[1], 16 * (ROUNDS - 1 + NB))

        @block.gpsimd
        def _(pool):
            ones = esum[:, 0:P]
            pool.memset(ones, 1.0).then_inc(pool_chain, 1)
            pool.memset(ident[:, :], 0.0).then_inc(pool_chain, 1)
            pool.memset(minus_r[:, :].bitcast(F32), -1.0).then_inc(const_done, 1)
            pool.wait_ge(pool_chain, 2)
            for dst, src, op, fill, cm, st in ((ident, ident[:, :], ALU.not_equal, 1.0, 1, -1),
                                               (low, ones, ALU.is_ge, 0.0, 1, -1),
                                               (below, ones, ALU.is_gt, 0.0, 1, -1),
                                               (above, ones, ALU.is_gt, 0.0, -1, 1)):
                pool.affine_select(out=dst[:, :], in_=src, compare_op=op, fill=fill, base=0,
                                   pattern=[[st, P]], channel_multiplier=cm).then_inc(const_done, 1)
            for x in range(2):
                pool.memset(hl_hi[x][:, :, H:VW].bitcast(F32), 1.0).then_inc(const_done, 1)
                pool.memset(hl_lo[x][:, :, H:VW].bitcast(F32), 0.0).then_inc(const_done, 1)
            pool.memset(hr_hi[1][:, :, H:VW].bitcast(F32), 1.0).then_inc(const_done, 1)
            pool.memset(hr_lo[1][:, :, H:VW].bitcast(F32), 0.0).then_inc(const_done, 1)

            def split_w(i, s, slot):
                n = w_index(i, s, slot)
                pool.wait_ge(w_split_hi, n + 1)
                pool.tensor_tensor(w_lo[:, slot, :, :], w_stage[:, :, :], w_hi[:, slot, :, :].bitcast(F32),
                                   ALU.subtract).then_inc(w_split_lo, 1)

            def values_lo(i, s, first, hi, lo, ks=range(NB)):
                for k in ks:
                    n = HL_BEFORE[s] + first + k
                    pool.wait_ge(proj_hi, i * 56 + (PHI_BEFORE[s] + (6 if s < 4 else 0) + first + k + 1))
                    pool.tensor_tensor(lo[:, k, 0:H], pt[:, n % 2, 0:H], hi[:, k, 0:H].bitcast(F32),
                                       ALU.subtract).then_inc(val_lo, 1)

            def weights_lo(i, s, J):
                pool.wait_ge(weight_hi, step_count(i, s, 4, J))
                w = S if s < 4 else DW
                pool.tensor_tensor(d_lo[:, J, 0:w], td[:, J % 3, 0:w], d_hi[:, J, 0:w].bitcast(F32),
                                   ALU.subtract).then_inc(weight_lo, 1)

            def weights_of(i, s, J):
                pool.wait_ge(exp_done, step_count(i, s, 4, J))
                t = td[:, J % 3, 0:S]
                pool.tensor_tensor(t, t, adjt[s % 2][:, J, :], ALU.mult).then_inc(weight_done, 1)

            def shift(i, s, bs=range(NB)):
                for b in bs:
                    if s == 4 and b > 2:
                        pool.wait_ge(normed, finished(i, s, b))
                        pool.tensor_tensor(xhat[:, b, :], xhat[:, b, :], vec[:, 2, :], ALU.mult).then_inc(scaled, 1)
                    pool.wait_ge(scaled, finished(i, s, b))
                    pool.tensor_tensor(xhat[:, b, :], xhat[:, b, :], vec[:, 3 if s in (3, 4) else 8, :],
                                       ALU.add).then_inc(shifted, 1)

            def self_bias(i, s, b):
                x = s % 2
                pool.wait_ge(ring_free, freed(i, s, "hs", b))
                pool.tensor_tensor(hs[x][:, b, :], hs[x][:, b, :], vec[:, 6, :], ALU.add).then_inc(hs_ready, 1)

            def exp_sum(i, s, J):
                pool.wait_ge(exp_done, step_count(i, s, 4, J))
                if J == 1:
                    if s == 5:
                        pool.wait_ge(ring_full, job(i, 5, "z"))
                    elif late(i, 0):
                        pool.wait_ge(ring_full, job(i, 0, "z"))
                    pool.tensor_tensor(esum[:, :], td[:, 0, 0:S], td[:, 1, 0:S], ALU.add).then_inc(esum_done, 2)
                else:
                    pool.wait_ge(esum_done, i * 8 + ((s - 4) * 4 + J))
                    pool.tensor_tensor(esum[:, :], esum[:, :], td[:, J % 3, 0:S], ALU.add).then_inc(esum_done, 1)

            def round_of_pool(i):
                for s in range(STEPS):
                    x = s % 2
                    if s < 4:
                        if s == 0:
                            split_w(i, s, 2)
                        if s == 1:
                            split_w(i, s + 1, 0)
                            split_w(i, s + 1, 1)
                        if s == 3:
                            shift(i, s)
                        values_lo(i, s, 0, hl_hi[x], hl_lo[x], range(2))
                        if s == 3:
                            split_w(i, s + 1, 0)
                        values_lo(i, s, 0, hl_hi[x], hl_lo[x], range(2, NB))
                        weights_of(i, s, 0)
                        weights_of(i, s, 1)
                        weights_lo(i, s, 0)
                        weights_lo(i, s, 1)
                        if s == 0 and late(i, s):
                            shift(i, s, range(2))
                        if s == 1:
                            split_w(i, s + 1, 2)
                        if s != 2:
                            weights_of(i, s, 2)
                            weights_of(i, s, 3)
                        weights_lo(i, s, 2)
                        weights_lo(i, s, 3)
                        if s == 0 and late(i, s):
                            shift(i, s, range(2, NB))
                    else:
                        values_lo(i, s, 0, hl_hi[x], hl_lo[x], range(2))
                        if s == 5:
                            self_bias(i, 4, 0)
                            self_bias(i, 4, 1)
                        values_lo(i, s, 0, hl_hi[x], hl_lo[x], range(2, NB))
                        if s == 5:
                            self_bias(i, 4, 2)
                            self_bias(i, 4, 3)
                        if s == 4:
                            split_w(i, s, 1)
                            split_w(i, s, 2)
                        else:
                            split_w(i, s + 1, 0)
                        shift(i, s)
                        values_lo(i, s, 4, hr_hi[x], hr_lo[x])
                        exp_sum(i, s, 1)
                        exp_sum(i, s, 2)
                        weights_lo(i, s, 0)
                        exp_sum(i, s, 3)
                        if s == 5:
                            split_w(i, s + 1, 1)
                        weights_lo(i, s, 1)
                        weights_lo(i, s, 2)
                        weights_lo(i, s, 3)
                        if s == 5:
                            for b in range(NB):
                                self_bias(i, s, b)

            split_w(0, 0, 0)
            split_w(0, 0, 1)
            round_of_pool(0)
            with pool.Fori(1, ROUNDS) as i:
                round_of_pool(i)
            shift(ROUNDS, 0)

        @block.scalar
        def _(act):
            def split_w(i, s, slot):
                n = w_index(i, s, slot)
                act.wait_ge(w_raw, n * 16 + 16)
                if not (isinstance(i, int) and i == 0 and s == 0):
                    q = s - 1
                    if q >= 0:
                        last = [("ml", 2), ("mr", 2), ("hl", 3)] if q < 4 else [("hl", 3), ("hr", 3), ("hs", 3)]
                        act.wait_ge(ring_full, job(i, q, *last[slot]))
                    else:
                        act.wait_ge(ring_full, i * JOBS_PER_ROUND)
                act.activation(w_hi[:, slot, :, :], w_stage[:, :, :], ACT.Copy).then_inc(w_split_hi, 1)

            def feature_hi(g_i, g_s, k):
                if g_s in (2, 3):
                    act.wait_ge(ht_pre, g_i * 6 + ((g_s - 2) * 3 + k + 1))
                    wait_ht_free(act, g_i, g_s, k)
                    src = pt[:, k % 2, :]
                    act.activation(ht_hi[:, k, :], src, ACT.Relu).then_inc(ht_hi_done, 1)
                    return
                if g_s in (0, 5):
                    act.wait_ge(ts_full, g_i * 6 + ((3 if g_s == 5 else 0) + k + 1))
                    src = score[k]
                else:
                    q = g_s - 1
                    act.wait_ge(ring_full, job(g_i, q, "t", k))
                    src = bank(q, "t", k)
                wait_ht_free(act, g_i, g_s, k)
                act.activation(ht_hi[:, k, :], src[:, :], ACT.Relu).then_inc(ht_hi_done, 1)

            def mixed_hi(i, s, name, ks=range(NC)):
                hi = ml_hi if name == "ml" else mr_hi
                for k in ks:
                    act.wait_ge(ring_full, job(i, s, name, k))
                    act.activation(hi[:, k, :], bank(s, name, k)[:, :], ACT.Copy).then_inc(proj_hi, 1)

            def values_hi(i, s, name, first, hi, ks=range(NB)):
                for k in ks:
                    n = HL_BEFORE[s] + first + k
                    act.wait_ge(ring_free, freed(i, s, name, k))
                    act.activation(hi[:, k, 0:H], pt[:, n % 2, 0:H], ACT.Copy).then_inc(proj_hi, 1)

            def exp_of(i, s, J):
                if s < 4:
                    act.wait_ge(masked, i * 16 + (s * 4 + J + 1))
                    act.activation(td[:, J % 3, 0:S], td[:, J % 3, 0:S], ACT.Exp).then_inc(exp_done, 1)
                else:
                    act.wait_ge(max_added, i * 8 + ((s - 4) * 4 + J + 1))
                    if J == 3:
                        act.wait_ge(weight_lo, step_count(i, s, 4, 0))
                    elif J == 0:
                        act.wait_ge(weight_lo, i * 24 + 4 * s)
                    act.activation(td[:, J % 3, 0:S], score[J][:, :], ACT.Exp, scale=ROOT_H).then_inc(exp_done, 1)

            def max_diag(i, s):
                if s == 5:
                    act.wait_ge(max_added, i * 8 + 4)
                elif late(i, 0):
                    act.wait_ge(max_added, i * 8)
                for J in range(NB):
                    act.wait_ge(max_ready, i * 8 + ((s - 4) * 4 + J + 1))
                    ins = act.activation(maxdiag[:, J, :], ident[:, :], ACT.Copy, scale=mx[:, J:J + 1])
                ins.then_inc(diag_ready, 1)

            def weight_hi_of(i, s, J):
                act.wait_ge(weight_done, step_count(i, s, 4, J))
                w = S if s < 4 else DW
                act.activation(d_hi[:, J, 0:w], td[:, J % 3, 0:w], ACT.Copy).then_inc(weight_hi, 1)

            def context_rows(i, s):
                if s == 0:
                    act.wait_ge(out_ready[0], i)
                elif s == 1 and late(i, 0):
                    act.wait_ge(out_ready[1], i)
                for b in range(NB):
                    act.wait_ge(sums_ready, contexts_read(i, s, b))
                    act.activation(xhat[:, b, :], bank(s, "c", b)[:, 0:H], ACT.Copy,
                                   scale=rden[:, b:b + 1]).then_inc(context_free, 1)

            def context_norm(i, s):
                act.wait_ge(context_scaled, i * STEPS + s)
                for b in range(NB):
                    act.activation(xhat[:, b, :], xhat[:, b, :], ACT.Identity, scale=ctx_rs[:, b:b + 1],
                                   bias=ctx_nb[:, b:b + 1]).then_inc(xhat_ready if s in (1, 2) else normed, 1)

            def self_values(i, s, bs):
                for b in bs:
                    act.wait_ge(ring_full, job(i, s, "hs", b))
                    act.activation(hs[s % 2][:, b, :], bank(s, "hs", b)[:, 0:H], ACT.Copy).then_inc(ring_free, 1)

            def pre_norm(n, src, dst, ready):
                act.wait_ge(pre_scaled, n)
                for b in range(NB):
                    act.activation(dst[:, b, :], src[:, b, :], ACT.Identity,
                                   scale=pre_rs[:, b:b + 1], bias=pre_nb[:, b:b + 1]).then_inc(ready, 1)

            def round_of_act(i):
                for s in range(STEPS):
                    x = s % 2
                    g_i, g_s = (i, s + 1) if s < 5 else (i + 1, 0)
                    if s in (1, 2):
                        mixed_hi(i, s, "ml")
                    if s in (1, 2, 3, 4):
                        weight_hi_of(i, s - 1, 2)
                        weight_hi_of(i, s - 1, 3)
                    if s < 4:
                        if s in (0, 3):
                            mixed_hi(i, s, "ml")
                        if s == 3:
                            context_rows(i, s)
                            mixed_hi(i, s, "mr", range(2))
                            context_norm(i, s)
                            mixed_hi(i, s, "mr", range(2, NC))
                        elif late(i, s):
                            mixed_hi(i, s, "mr")
                        else:
                            mixed_hi(i, s, "mr", range(2))
                        if s == 0:
                            split_w(i, s, 2)
                        if not late(i, s):
                            mixed_hi(i, s, "mr", range(2, NC))
                        if x == 1:
                            split_w(i, s + 1, 0)
                        if s == 2:
                            pre_norm(prenorms(i, s), xnext, xnext, xnext_ready)
                        if s < 3 and late(i, s):
                            context_rows(i, s)
                        if s == 1:
                            split_w(i, s + 1, 1)
                        values_hi(i, s, "hl", 0, hl_hi[x], range(2))
                        if s < 3 and late(i, s):
                            context_norm(i, s)
                        if s == 3:
                            values_hi(i, s, "hl", 0, hl_hi[x], [2])
                            exp_of(i, s, 0)
                            values_hi(i, s, "hl", 0, hl_hi[x], [3])
                            exp_of(i, s, 1)
                            pre_norm(prenorms(i, s), xres[0], xhat, xhat_ready)
                            weight_hi_of(i, s, 0)
                            feature_hi(g_i, g_s, 0)
                            feature_hi(g_i, g_s, 1)
                            weight_hi_of(i, s, 1)
                        else:
                            values_hi(i, s, "hl", 0, hl_hi[x], range(2, NB))
                            exp_of(i, s, 0)
                            if s == 0:
                                pre_norm(prenorms(i, s), xnext, xnext, xnext_ready)
                            exp_of(i, s, 1)
                            weight_hi_of(i, s, 0)
                            weight_hi_of(i, s, 1)
                            if s == 1:
                                split_w(i, s + 1, 2)
                            feature_hi(g_i, g_s, 0)
                            feature_hi(g_i, g_s, 1)
                        feature_hi(g_i, g_s, 2)
                        exp_of(i, s, 2)
                        exp_of(i, s, 3)
                    else:
                        values_hi(i, s, "hl", 0, hl_hi[x])
                        if s == 4:
                            split_w(i, s, 1)
                        context_rows(i, s)
                        if s == 4:
                            split_w(i, s, 2)
                        else:
                            split_w(i, s + 1, 0)
                        context_norm(i, s)
                        max_diag(i, s)
                        values_hi(i, s, "hr", 4, hr_hi[x])
                        if s == 5:
                            split_w(i, s + 1, 1)
                        exp_of(i, s, 0)
                        exp_of(i, s, 1)
                        exp_of(i, s, 2)
                        if s == 4:
                            pre_norm(prenorms(i, s), xres[1], xhat, xhat_ready)
                            weight_hi_of(i, s, 0)
                        feature_hi(g_i, g_s, 0)
                        feature_hi(g_i, g_s, 1)
                        if s == 5:
                            weight_hi_of(i, s, 0)
                        self_values(i, s, range(NB))
                        feature_hi(g_i, g_s, 2)
                        exp_of(i, s, 3)
                        weight_hi_of(i, s, 1)
                        weight_hi_of(i, s, 2)
                        weight_hi_of(i, s, 3)

            pre_norm(1, xnext, xnext, xnext_ready)
            split_w(0, 0, 0)
            for k in range(NC):
                feature_hi(0, 0, k)
            split_w(0, 0, 1)
            round_of_act(0)
            with act.Fori(1, ROUNDS) as i:
                round_of_act(i)
            context_rows(ROUNDS, 0)
            context_norm(ROUNDS, 0)

        @block.tensor
        def _(pe):
            def mm3(dst, a, b, start, stop):
                pe.matmul(dst, a[0], b[0], start=start, stop=False)
                pe.matmul(dst, a[0], b[1], start=False, stop=False)
                return pe.matmul(dst, a[1], b[0], start=False, stop=stop)

            def feat(k, lo, hi):
                return ht_hi[:, k, lo:hi], ht_lo[:, k, lo:hi]

            def weight(slot, k, lo=0, hi=H):
                return w_hi[:, slot, k, lo:hi], w_lo[:, slot, k, lo:hi]

            def wait_bank(i, s, name, k=0):
                n = JOBS[s, name, k]
                if left_out(i) and n - 4 < left_out(i):
                    pe.wait_ge(ring_free, ROUNDS * len(FREES))
                    return
                if n < 4:
                    if isinstance(i, int) and i == 0:
                        return
                    before = max(m for m in range(JOBS_PER_ROUND - 4, JOBS_PER_ROUND) if m % 4 == n)
                    pe.wait_ge(ring_free, freed(i, *JOB_AT[before]) - len(FREES))
                    return
                q, what, c = JOB_AT[n - 4]
                if what == "t":
                    pe.wait_ge(ht_lo_done, step_count(i, q + 1, 3, c))
                elif what == "c":
                    if late(i, q):
                        pe.wait_ge(context_free, contexts_read(i, q, c))
                    else:
                        pe.wait_ge(ring_free, freed(i, q, "mr", NC - 1))
                else:
                    pe.wait_ge(ring_free, freed(i, q, what, c))

            def wait_feat(i, s, k):
                pe.wait_ge(ht_hi_done, step_count(i, s, 3, k))
                pe.wait_ge(ht_lo_done, step_count(i, s, 3, k))

            def wait_weight(i, s, slot):
                pe.wait_ge(w_split_lo, w_index(i, s, slot) + 1)

            def mix_keys(i, s, name, slot, outer):
                wait_weight(i, s, slot)
                if outer:
                    for k in range(NC):
                        wait_feat(i, s, k)
                        for c in range(NC):
                            if k == 0:
                                wait_bank(i, s, name, c)
                            m = mm3(bank(s, name, c)[:, :], weight(slot, k, c * P, (c + 1) * P), feat(k, 0, S),
                                    k == 0, k == NC - 1)
                            if k == NC - 1:
                                m.then_inc(ring_full, 1)
                    return
                for c in range(NC):
                    wait_bank(i, s, name, c)
                    for k in range(NC):
                        m = mm3(bank(s, name, c)[:, :], weight(slot, k, c * P, (c + 1) * P), feat(k, 0, S),
                                k == 0, k == NC - 1)
                    m.then_inc(ring_full, 1 if late(i, s) or c < NC - 1 else 1 + 1 + NB)

            def values(i, s, name, slot):
                wait_weight(i, s, slot)
                for b in range(NB):
                    wait_bank(i, s, name, b)
                    for k in range(NC):
                        m = mm3(bank(s, name, b)[:, 0:H], feat(k, b * P, (b + 1) * P), weight(slot, k),
                                k == 0, k == NC - 1)
                    m.then_inc(ring_full, 1)

            def values_outer(i, s, name, slot, ks, free_feat):
                for k in ks:
                    if k == 0:
                        wait_weight(i, s, slot)
                    if not free_feat:
                        wait_feat(i, s, k)
                    for b in range(NB):
                        if k == 0:
                            wait_bank(i, s, name, b)
                        m = mm3(bank(s, name, b)[:, 0:H], feat(k, b * P, (b + 1) * P), weight(slot, k),
                                k == 0, k == NC - 1)
                        if k == NC - 1:
                            m.then_inc(ring_full, 1)
                    if free_feat and k < NC - 1:
                        m.then_inc(ht_free, 1)

            def exp_sums(i, s):
                wait_bank(i, s, "z")
                pe.wait_ge(esum_done, (i * 8 + 4) if s == 5 else i * 8)
                for b in range(NB):
                    m = pe.matmul(bank(s, "z")[:, b:b + 1], esum[:, b * P:(b + 1) * P],
                                  minus_r[:, 0:1].bitcast(F32), start=True, stop=True)
                m.then_inc(ring_full, 1)

            def context(i, s):
                q = (s - 1) % STEPS
                x = q % 2
                qi = i if s else i - 1
                values_before = (qi * 32) + HL_BEFORE[q] + (4 if q < 4 else 8)
                pe.wait_ge(val_lo, values_before)
                for b in range(NB):
                    wait_bank(i, s, "c", b)
                    terms = []
                    for J in range(NB):
                        cols = slice(b * P, (b + 1) * P)
                        if q < 4 or J > b:
                            terms.append((J, cols, hl_hi[x], hl_lo[x]))
                        elif J == b:
                            terms.append((J, cols, hl_hi[x], hl_lo[x]))
                            terms.append((J, slice(S, DW), hr_hi[x], hr_lo[x]))
                        else:
                            terms.append((J, cols, hr_hi[x], hr_lo[x]))
                    for n, (J, cols, vh, vl) in enumerate(terms):
                        if b == 0:
                            pe.wait_ge(weight_lo, step_count(qi, q, 4, J))
                        m = mm3(bank(s, "c", b)[:, 0:VW], (d_hi[:, J, cols], d_lo[:, J, cols]),
                                (vh[:, J, :], vl[:, J, :]), n == 0, n == len(terms) - 1)
                    m.then_inc(ring_full, 1)
                    if s == 5 and b == 0:
                        exp_sums(i, s)

            def transposes(i, s, dst, full, wait_dst):
                src = xnext if s in (5, 0, -1) else xhat
                for b in range(NB):
                    if src is xnext:
                        pe.wait_ge(xnext_ready, b + 1 if s == -1 else next_ready(i, s, b))
                    else:
                        pe.wait_ge(xhat_ready, rows_ready(i, s, b))
                    for k in range(NC):
                        if b == 0:
                            wait_dst(k)
                        m = pe.transpose(dst[k][:, b * P:(b + 1) * P], src[:, b, k * P:(k + 1) * P], ident[:, :])
                        if b == NB - 1:
                            m.then_inc(full, 1)

            def edge_scores(i, s, J, ks, free):
                left, right = score[2 * (J % 2)], score[2 * (J % 2) + 1]
                lw = max(MIN_N, (J + 1) * P)
                rl = min(S - MIN_N, J * P)
                for k in ks:
                    mm3(left[:, 0:lw], (ml_hi[:, k, J * P:(J + 1) * P], ml_lo[:, k, J * P:(J + 1) * P]),
                        feat(k, 0, lw), k == 0, k == NC - 1)
                    m = mm3(right[:, rl:S], (mr_hi[:, k, J * P:(J + 1) * P], mr_lo[:, k, J * P:(J + 1) * P]),
                            feat(k, rl, S), k == 0, k == NC - 1)
                    if k == NC - 1:
                        m.then_inc(score_full, 1)
                    elif free:
                        m.then_inc(ht_free, 1)

            def edge_step(i, s):
                mix_keys(i, s, "ml", 0, True)
                if s == 3:
                    context(i, s)
                mix_keys(i, s, "mr", 1, False)
                if s < 3 and late(i, s):
                    if s == 0:
                        exp_sums(i, s)
                    context(i, s)
                values(i, s, "hl", 2)
                pe.wait_ge(ring_free, freed(i, s, "mr", 2))
                if s > 0:
                    pe.wait_ge(masked, i * 16 + 4 * s)
                else:
                    if late(i, s):
                        pe.wait_ge(exp_done, i * 24)
                    pe.wait_ge(ht_lo_done, i * 18 + 3)
                edge_scores(i, s, 0, range(NC), False)
                edge_scores(i, s, 1, range(NC), False)
                for k in range(NC):
                    if k == 0:
                        pe.wait_ge(masked, i * 16 + (4 * s + 1))
                    edge_scores(i, s, 2, [k], False)
                    if k == 0:
                        pe.wait_ge(masked, i * 16 + (4 * s + 2))
                    edge_scores(i, s, 3, [k], True)
                    if k == (1 if s == 3 else 0):
                        transposes(i, s, [bank(s, "t", c) for c in range(NC)], ring_full,
                                   lambda c: wait_bank(i, s, "t", c))

            def soft_step(i, s):
                values_outer(i, s, "hl", 0, range(NC), False)
                context(i, s)
                if s == 4:
                    pe.wait_ge(masked, i * 16 + 16)
                else:
                    pe.wait_ge(exp_done, i * 24 + 20)
                    pe.wait_ge(ht_lo_done, i * 18 + 18)
                for J in range(NB):
                    for k in range(NC):
                        m = mm3(score[J][:, :], feat(k, J * P, (J + 1) * P), feat(k, 0, S), k == 0, k == NC - 1)
                    m.then_inc(score_full, 1)
                values(i, s, "hr", 1)
                pe.wait_ge(diag_ready, i * 2 + (s - 3))
                for J in range(NB):
                    pe.matmul(score[J][:, :], minus_r[:, :], maxdiag[:, :, :].rearrange("p b q -> p (b q)"),
                              start=False, stop=True, skip_group_check=True).then_inc(max_added, 1)
                values_outer(i, s, "hs", 2, range(NC - 1), True)
                transposes(i, s, score, ts_full, lambda c: pe.wait_ge(exp_done, step_count(i, s, 4, c)))
                values_outer(i, s, "hs", 2, [NC - 1], True)

            def round_of_pe(i):
                for s in range(4):
                    edge_step(i, s)
                for s in range(4, STEPS):
                    soft_step(i, s)

            pe.wait_ge(const_done, 11)
            transposes(0, -1, score, ts_full, lambda c: None)
            round_of_pe(0)
            with pe.Fori(1, ROUNDS) as i:
                round_of_pe(i)
            exp_sums(ROUNDS, 0)
            context(ROUNDS, 0)

        @block.vector
        def _(dve):
            chain = {"base": 0, "n": 0}

            def link(ins):
                ins.then_inc(dve_chain, 1)
                chain["n"] += 1
                dve.wait_ge(dve_chain, chain["base"] + chain["n"])

            def rsqrt(dst):
                link(dve.tensor_scalar(nt.bitcast(I32), var.bitcast(I32), 1, None, ALU.logical_shift_right))
                link(dve.tensor_scalar(dst.bitcast(I32), nt.bitcast(I32), -1.0, RSQRT_GUESS, ALU.mult, ALU.add))
                for _ in range(3):
                    link(dve.tensor_tensor(nt, dst, dst, ALU.mult))
                    link(dve.scalar_tensor_tensor(nt, nt, -0.5, var, ALU.mult, ALU.mult))
                    link(dve.scalar_tensor_tensor(dst, nt, 1.5, dst, ALU.add, ALU.mult))

            def row_moments(st=stats):
                mean_e, mean_o, ssd_e, ssd_o = (st[:, :, q] for q in (1, 4, 2, 5))
                dve.tensor_tensor(msum, mean_e, mean_o, ALU.add).then_inc(dve_chain, 1)
                dve.tensor_tensor(nt, mean_e, mean_o, ALU.subtract).then_inc(dve_chain, 1)
                chain["n"] += 2
                link(dve.tensor_tensor(var, ssd_e, ssd_o, ALU.add))
                link(dve.scalar_tensor_tensor(nt, nt, 0.25, nt, ALU.mult, ALU.mult))
                link(dve.scalar_tensor_tensor(var, var, 1.0 / H, nt, ALU.mult, ALU.add))

            def pre_moments(st=stats):
                row_moments(st)
                link(dve.tensor_scalar(var, var, 1e-5, None, ALU.add))

            def pre_scale():
                rsqrt(pre_rs)
                dve.scalar_tensor_tensor(pre_nb, msum, -0.5, pre_rs, ALU.mult, ALU.mult).then_inc(pre_scaled, 1)

            def load_stats(n):
                dve.wait_ge(xnext_in, n)
                for b in range(NB):
                    ins = dve.bn_stats(stats_in[:, b, :], xnext[:, b, :])
                link(ins)

            def edge_rows(i, s):
                if not (isinstance(i, int) and i == 0 and s == 1):
                    dve.wait_ge(context_free, contexts_read(i, s - 1, NB - 1))
                for b in range(NB):
                    src = bank(s, "c", b)
                    dve.wait_ge(ring_full, job(i, s, "c", b))
                    link(dve.tensor_scalar(den[:, b:b + 1], src[:, H:H + 1], 1e-10, None, ALU.add))
                    dve.reciprocal(rden[:, b:b + 1], den[:, b:b + 1]).then_inc(sums_ready, 1)
                    if b > 0:
                        dve.wait_ge(context_free, contexts_read(i, s, b - 1))
                        dve.bn_stats(stats[:, b - 1, :], xhat[:, b - 1, :])
                dve.wait_ge(context_free, contexts_read(i, s, NB - 1))
                link(dve.bn_stats(stats[:, NB - 1, :], xhat[:, NB - 1, :]))

            def edge_scale(i, s):
                row_moments()
                link(dve.tensor_scalar(var, var, H / (H - 1.0), 1e-30, ALU.mult, ALU.max))
                rsqrt(den)
                link(dve.tensor_tensor(nt, var, den, ALU.mult))
                link(dve.tensor_scalar(nt, nt, 1e-3, None, ALU.add))
                if s == 1:
                    if late(i, 0):
                        dve.wait_ge(normed, finished(i, 0, NB - 1))
                elif s in (2, 3):
                    dve.wait_ge(xhat_ready, rows_ready(i, s - 1, NB - 1))
                else:
                    dve.wait_ge(normed, finished(i, s - 1, NB - 1))
                link(dve.reciprocal(ctx_rs, nt))
                dve.scalar_tensor_tensor(ctx_nb, msum, -0.5, ctx_rs, ALU.mult, ALU.mult).then_inc(context_scaled, 1)

            def scale(i, s, b):
                dve.wait_ge(normed, finished(i, s, b))
                dve.tensor_tensor(xhat[:, b, :], xhat[:, b, :], vec[:, 2 if s in (3, 4) else 7, :],
                                  ALU.mult).then_inc(scaled, 1)

            def residual(i, s, bs=range(NB)):
                x = (s - 1) % 2
                for b in bs:
                    if b == 0 and s in (3, 4):
                        dve.wait_ge(xres_in[x], i * 16 + 16)
                    dve.wait_ge(shifted, finished(i, s, b))
                    ins = dve.scalar_tensor_tensor(xres[x][:, b, :], xhat[:, b, :], 0.0, xres[x][:, b, :],
                                                   ALU.max, ALU.add)
                    if s in (3, 4):
                        link(ins)
                        ins = dve.bn_stats(stats[:, b, :], xres[x][:, b, :])
                        if b == NB - 1:
                            link(ins)
                    elif b == NB - 1 or (isinstance(i, int) and i == ROUNDS):
                        ins.then_inc(out_ready[x], 1)

            def soft_rows(i, s):
                x = (s - 1) % 2
                dd = diag[:, x, :]
                dve.wait_ge(ring_full, job(i, s, "z"))
                dve.tensor_copy(zc, bank(s, "z")[:, 0:NB]).then_inc(ring_free, 1)
                dve.wait_ge(ring_free, freed(i, s, "z"))
                dve.wait_ge(context_free, contexts_read(i, s, 0) - 1)
                for b in range(NB + 1):
                    if b < NB:
                        src = bank(s, "c", b)
                        c = slice(b, b + 1)
                        dve.wait_ge(ring_full, job(i, s, "c", b))
                        link(dve.scalar_tensor_tensor(den[:, c], zc[:, c], -1e-10, src[:, H:H + 1], ALU.mult, ALU.add))
                        link(dve.tensor_tensor(den[:, c], den[:, c], dd[:, c], ALU.add))
                        dve.reciprocal(rden[:, c], den[:, c]).then_inc(sums_ready, 1)
                        dve.wait_ge(sums_ready, contexts_read(i, s, b))
                        link(dve.tensor_tensor(ddr[:, c], dd[:, c], rden[:, c], ALU.mult))
                    if b > 0:
                        c = slice(b - 1, b)
                        dve.wait_ge(hs_ready, i * 8 + ((b if s == 5 else b - NB)))
                        dve.wait_ge(context_free, contexts_read(i, s, b - 1))
                        link(dve.scalar_tensor_tensor(xhat[:, b - 1, :], hs[x][:, b - 1, :], ddr[:, c],
                                                      xhat[:, b - 1, :], ALU.mult, ALU.add))
                        ins = dve.bn_stats(stats[:, b - 1, :], xhat[:, b - 1, :])
                link(ins)

            def soft_scale(i, s):
                row_moments()
                link(dve.tensor_scalar(var, var, 1e-12, None, ALU.add))
                dve.wait_ge(normed, finished(i, s, 0) - 1)
                rsqrt(ctx_rs)
                dve.scalar_tensor_tensor(ctx_nb, msum, -0.5, ctx_rs, ALU.mult, ALU.mult).then_inc(context_scaled, 1)

            def feature_pre(g_i, g_s, k):
                src = bank(g_s - 1, "t", k)
                dve.wait_ge(ring_full, job(g_i, g_s - 1, "t", k))
                if k < 2:
                    dve.wait_ge(val_lo, g_i * 32 + (HL_BEFORE[g_s]))
                else:
                    dve.wait_ge(ht_lo_done, step_count(g_i, g_s, 3, 0))
                dve.tensor_scalar(pt[:, k % 2, :], src[:, :], lnab[:, 0, k:k + 1], lnab[:, 1, k:k + 1],
                                  ALU.mult, ALU.add).then_inc(ht_pre, 1)

            def feature_lo(g_i, g_s, k):
                dve.wait_ge(ht_hi_done, step_count(g_i, g_s, 3, k))
                if g_s in (2, 3):
                    src = pt[:, k % 2, :]
                else:
                    src = (bank(g_s - 1, "t", k) if g_s not in (0, 5) else score[k])[:, :]
                dve.scalar_tensor_tensor(ht_lo[:, k, :], src, 0.0, ht_hi[:, k, :].bitcast(F32),
                                         ALU.max, ALU.subtract).then_inc(ht_lo_done, 1)

            def mixed_lo(i, s, name, ks=range(NC)):
                first, hi, lo = (0, ml_hi, ml_lo) if name == "ml" else (NC, mr_hi, mr_lo)
                for k in ks:
                    dve.wait_ge(proj_hi, i * 56 + (PHI_BEFORE[s] + first + k + 1))
                    skipped = 0 if late(i, s) or name == "ml" or k < NC - 1 else 1
                    dve.tensor_tensor(lo[:, k, :], bank(s, name, k)[:, :], hi[:, k, :].bitcast(F32),
                                      ALU.subtract).then_inc(ring_free, 1 + skipped)

            def values_bias(i, s, name, first, bias, ks=range(NB)):
                for k in ks:
                    n = HL_BEFORE[s] + first + k
                    dve.wait_ge(ring_full, job(i, s, name, k))
                    if not (isinstance(i, int) and i == 0 and n < 2):
                        dve.wait_ge(val_lo, i * 32 + (n - 1))
                    dve.tensor_tensor(pt[:, n % 2, 0:H], bank(s, name, k)[:, 0:H], vec[:, bias, :],
                                      ALU.add).then_inc(ring_free, 1)

            def mask_of(i, s, J):
                x = s % 2
                left, right = score[2 * (J % 2)], score[2 * (J % 2) + 1]
                lo, hi = J * P, (J + 1) * P
                t = td[:, J % 3, :]
                dve.wait_ge(score_full, step_count(i, s, 4, J))
                if J == 0 and not (isinstance(i, int) and i == 0 and s == 0):
                    dve.wait_ge(weight_lo, i * 24 + 4 * s)
                elif J == 3:
                    dve.wait_ge(weight_lo, step_count(i, s, 4, 0))
                if J > 0:
                    dve.scalar_tensor_tensor(t[:, 0:lo], left[:, 0:lo], ROOT_H, adjt[x][:, J, 0:lo], ALU.mult, ALU.mult)
                    rest = slice(lo, S)
                else:
                    dve.scalar_tensor_tensor(t[:, P:S], right[:, P:S], ROOT_H, adjn[x][:, P:S], ALU.mult, ALU.mult)
                    rest = slice(0, P)
                link(dve.copy_predicated(right[:, lo:hi], low[:, :].bitcast(I32), left[:, lo:hi]))
                dve.scalar_tensor_tensor(t[:, rest], right[:, rest], ROOT_H,
                                         adjn[x][:, AT[J]:AT[J] + rest.stop - rest.start],
                                         ALU.mult, ALU.mult).then_inc(masked, 1)

            def weight_of(i, s, J):
                x = s % 2
                t = td[:, J % 3, :]
                lo, hi = J * P, (J + 1) * P
                dve.wait_ge(esum_done, i * 8 + ((s - 4) * 4 + max(J + 1, 2)))
                link(dve.tensor_tensor(t[:, 0:S], t[:, 0:S], adjt[x][:, J, :], ALU.mult))
                link(dve.scalar_tensor_tensor(t[:, S:DW], t[:, lo:hi], 1.0, ident[:, :], ALU.mult, ALU.mult,
                                              accum_out=diag[:, x, J:J + 1]))
                link(dve.tensor_tensor(t[:, S:DW], t[:, lo:hi], above[:, :], ALU.mult))
                dve.tensor_tensor(t[:, lo:hi], t[:, lo:hi], below[:, :], ALU.mult).then_inc(weight_done, 1)

            def maximum(i, s, J):
                if J == 0:
                    if s == 5:
                        dve.wait_ge(diag_ready, i * 2 + 1)
                    elif late(i, 0):
                        dve.wait_ge(diag_ready, i * 2)
                dve.wait_ge(score_full, step_count(i, s, 4, J))
                dve.tensor_reduce(mx[:, J:J + 1], score[J][:, :], AX_X, ALU.max).then_inc(max_ready, 1)

            def mirror_adj(i, x):
                for J in range(NB):
                    ins = dve.copy_predicated(adjn[x][:, AT[J]:AT[J] + P], low[:, :].bitcast(I32),
                                              adjt[x][:, J, J * P:(J + 1) * P])
                link(ins)

            def round_of_dve(i):
                for s in range(STEPS):
                    x = s % 2
                    g_i, g_s = (i, s + 1) if s < 5 else (i + 1, 0)
                    if s < 4:
                        if s == 0:
                            load_stats(i * 32 + 32)
                        elif s == 2:
                            load_stats(i * 32 + 48)
                        mixed_lo(i, s, "ml")
                        if s == 0 and not late(i, s):
                            mixed_lo(i, s, "mr")
                            dve.wait_ge(vec_in_sem, 32)
                        if s == 1 and late(i, 0):
                            residual(i, 0)
                        if s < 2:
                            dve.wait_ge(adj_in_sem[x], i * 80 + 80)
                        elif s == 2:
                            dve.wait_ge(xnext_ready, next_ready(i, 0, NB - 1))
                            pre_moments(stats_in)
                            pre_scale()
                        if s != 3 and late(i, s):
                            mixed_lo(i, s, "mr")
                        if s == 0:
                            if late(i, s):
                                dve.wait_ge(xhat_ready, i * 16)
                            else:
                                dve.wait_ge(xnext_ready, NB)
                            pre_moments(stats_in)
                            pre_scale()
                        if s < 2:
                            mirror_adj(i, x)
                        if s > 0:
                            edge_rows(i, s)
                            edge_scale(i, s)
                        elif late(i, s):
                            soft_rows(i, s)
                            soft_scale(i, s)
                        if s == 3:
                            mixed_lo(i, s, "mr", range(2))
                            for b in range(NB):
                                scale(i, s, b)
                            mixed_lo(i, s, "mr", range(2, NC))
                        values_bias(i, s, "hl", 0, s // 2, range(2))
                        if s == 3:
                            residual(i, s)
                        if s in (0, 1, 2):
                            values_bias(i, s, "hl", 0, s // 2, range(2, NB))
                        mask_of(i, s, 0)
                        if s == 3:
                            values_bias(i, s, "hl", 0, s // 2, range(2, NB))
                            pre_moments()
                        mask_of(i, s, 1)
                        if s == 3:
                            dve.wait_ge(xnext_ready, next_ready(i, 5, NB - 1))
                            pre_scale()
                        if s == 0 and late(i, s):
                            for b in range(NB):
                                scale(i, s, b)
                        for k in range(2):
                            if g_s in (2, 3):
                                feature_pre(g_i, g_s, k)
                            feature_lo(g_i, g_s, k)
                        if g_s in (2, 3):
                            feature_pre(g_i, g_s, 2)
                        mask_of(i, s, 2)
                        feature_lo(g_i, g_s, 2)
                        mask_of(i, s, 3)
                        if s == 2:
                            for J in (2, 3):
                                dve.wait_ge(exp_done, step_count(i, s, 4, J))
                                dve.tensor_tensor(td[:, J % 3, 0:S], td[:, J % 3, 0:S], adjt[x][:, J, :],
                                                  ALU.mult).then_inc(weight_done, 1)
                    else:
                        values_bias(i, s, "hl", 0, 4)
                        if s == 4:
                            link(dve.memset(hr_hi[0][:, :, H:VW].bitcast(F32), 1.0))
                            link(dve.memset(hr_lo[0][:, :, H:VW].bitcast(F32), 0.0))
                            edge_rows(i, s)
                            edge_scale(i, s)
                        else:
                            soft_rows(i, s)
                            soft_scale(i, s)
                        maximum(i, s, 0)
                        maximum(i, s, 1)
                        for b in range(3 if s == 4 else NB):
                            scale(i, s, b)
                        for J in (2, 3):
                            if s == 4:
                                residual(i, s, [J - 2])
                            maximum(i, s, J)
                        values_bias(i, s, "hr", 4, 5, range(2))
                        if s == 4:
                            residual(i, s, [2])
                        values_bias(i, s, "hr", 4, 5, [2])
                        if s == 4:
                            residual(i, s, [3])
                        if s == 4:
                            pre_moments()
                        values_bias(i, s, "hr", 4, 5, [3])
                        if s == 4:
                            dve.wait_ge(xhat_ready, rows_ready(i, 3, NB - 1))
                            pre_scale()
                        else:
                            residual(i, s)
                        weight_of(i, s, 0)
                        feature_lo(g_i, g_s, 0)
                        feature_lo(g_i, g_s, 1)
                        weight_of(i, s, 1)
                        feature_lo(g_i, g_s, 2)
                        weight_of(i, s, 2)
                        weight_of(i, s, 3)

            dve.wait_ge(const_done, 11)
            load_stats(16)
            pre_moments(stats_in)
            pre_scale()
            for k in range(NC):
                feature_lo(0, 0, k)
            round_of_dve(0)
            after_first = chain["n"]
            chain["n"] = 0
            per_round = DVE_LINKS
            with dve.Fori(1, ROUNDS) as i:
                chain["base"] = i * per_round + (after_first - per_round)
                round_of_dve(i)
            assert chain["n"] == per_round, chain["n"]
            chain["base"] = after_first + (ROUNDS - 1) * per_round
            chain["n"] = 0
            soft_rows(ROUNDS, 0)
            soft_scale(ROUNDS, 0)
            for b in range(NB):
                scale(ROUNDS, 0, b)
            residual(ROUNDS, 0)


DVE_LINKS = 292


def kernel(x, adj, L0_gnn_W_left, L0_gnn_W_right, L0_gnn_W_lin, L0_gnn_b_lin, L0_gnn_ln_a, L0_gnn_ln_b,
           L1_gnn_W_left, L1_gnn_b_left, L1_gnn_W_self, L1_gnn_b_self, L1_gnn_W_right, L1_gnn_b_right,
           L1_gnn_gamma, L1_gnn_beta):
    import numpy as np
    import concourse.bacc as bacc
    from concourse.bass_utils import run_bass_kernel_spmd

    f = np.ascontiguousarray
    w = f(np.stack([np.swapaxes(np.asarray(m), 0, 1) for m in (
        L0_gnn_W_left[0], L0_gnn_W_right[0], L0_gnn_W_lin[0],
        L0_gnn_W_left[1], L0_gnn_W_right[1], L0_gnn_W_lin[1],
        L1_gnn_W_left, L1_gnn_W_right, L1_gnn_W_self)]).reshape(3, 3, H, H))
    vec = np.stack([np.asarray(v) for v in (
        L0_gnn_b_lin[0], L0_gnn_b_lin[1], L0_gnn_ln_a[1], L0_gnn_ln_b[1],
        L1_gnn_b_left, L1_gnn_b_right, L1_gnn_b_self, L1_gnn_gamma, L1_gnn_beta)])
    vec = f(np.broadcast_to(vec[None], (P, 9, H)))
    lnab = f(np.stack([np.asarray(L0_gnn_ln_a[0]).reshape(NC, P),
                       np.asarray(L0_gnn_ln_b[0]).reshape(NC, P)]).transpose(2, 0, 1))
    arrays = {"x": f(x), "adj": f(adj), "adjt": f(np.swapaxes(np.asarray(adj), 1, 2)), "w": w, "vec": vec,
              "lnab": lnab}
    nc = bacc.Bacc("TRN2", target_bir_lowering=False, num_devices=1)
    args = [nc.dram_tensor(f"in_{n}", a.shape, mybir.dt.from_np(a.dtype), kind="ExternalInput").ap()
            for n, a in arrays.items()]
    out = nc.dram_tensor("out", (B, S, H), F32, kind="ExternalOutput").ap()
    gnn_kernel(nc, *args, out)
    r = run_bass_kernel_spmd(nc, [{f"in_{n}": a for n, a in arrays.items()}], core_ids=[0])
    return r.results[0]["out"]
```
